# Optimizing a Trainium2 kernel written in Bass

```python
import numpy as np
import jax
import jax.numpy as jnp

def _softmax(x, axis=-1):
    return jax.nn.softmax(x, axis=axis)

def _gelu(x):
    return jax.nn.gelu(x, approximate=True)

def _silu(x):
    return jax.nn.silu(x)

def _sigmoid(x):
    return jax.nn.sigmoid(x)

def _layernorm(x, axis=-1, eps=1e-05):
    m = jnp.mean(x, axis=axis, keepdims=True)
    v = jnp.var(x, axis=axis, keepdims=True)
    return (x - m) / jnp.sqrt(v + eps)

def _scatter_add(tgt, idx, src, axis=0):
    return tgt.at[idx].add(src)

def _segment_sum(src, seg, n):
    return jax.ops.segment_sum(src, seg, n)
kernel_name = 'mk_decoder_preln_d1_seqx_r8_3f6fa4'

def setup_inputs(seed: int=0):
    np.random.seed(seed)
    _w = jnp.asarray

    def _rec_inputs():
        import jax
        import jax.numpy as jnp
        _rk = jax.random.key(seed)
        x = 0.0002417 + 0.9998 * jax.random.normal(jax.random.fold_in(_rk, 1), (16, 256, 128), jnp.float32)
        _lenS = 256 - jax.random.randint(jax.random.fold_in(_rk, 7), (16,), 0, max(1, 256 // 4) + 1, jnp.int32)
        _lenS2 = 64 - jax.random.randint(jax.random.fold_in(_rk, 8), (16,), 0, max(1, 64 // 4) + 1, jnp.int32)
        _ctx_1024P = jax.random.normal(jax.random.fold_in(_rk, 11), (16, 16, 128), jnp.float32)
        _ctx_1024c = jax.random.dirichlet(jax.random.fold_in(_rk, 511), 0.3 * jnp.ones((16,), jnp.float32), (16, 64))
        _ctx_1024t = jnp.einsum('bsk,bkd->bsd', _ctx_1024c, _ctx_1024P)
        _ctx_1024t = _ctx_1024t * jax.lax.rsqrt(jnp.mean(jnp.square(_ctx_1024t)) + 1e-12) * 0.953939
        ctx_1024 = 7.22013e-05 + 1.00017 * (_ctx_1024t + 0.3 * jax.random.normal(jax.random.fold_in(_rk, 611), (16, 64, 128), jnp.float32))
        return (x, ctx_1024)
    x, ctx_1024 = _rec_inputs()

    def _L0_attn_setup():
        import jax, jax.numpy as jnp
        import numpy as np
        NUM_HEADS = 16
        LN_EPS = 1e-05
        key = jax.random.key(seed)
        ks = jax.random.split(key, 5)
        B, S, E = (4, 128, 128)
        x = jax.random.normal(ks[0], (B, S, E), dtype=jnp.float32)
        Wq = jax.random.normal(ks[1], (E, E), dtype=jnp.float32) * E ** (-0.5)
        Wk = jax.random.normal(ks[2], (E, E), dtype=jnp.float32) * E ** (-0.5)
        Wv = jax.random.normal(ks[3], (E, E), dtype=jnp.float32) * E ** (-0.5)
        Wo = jax.random.normal(ks[4], (E, E), dtype=jnp.float32) * E ** (-0.5)
        gamma = jnp.ones((E,), dtype=jnp.float32)
        beta = jnp.zeros((E,), dtype=jnp.float32)
        return {'x': x, 'Wq': Wq, 'Wk': Wk, 'Wv': Wv, 'Wo': Wo, 'gamma': gamma, 'beta': beta}
    _L0_attn_all = _L0_attn_setup()
    _L0_attn_in = {k: v for k, v in _L0_attn_all.items() if k in ('Wq', 'Wk', 'Wv', 'Wo', 'gamma', 'beta')}
    del _L0_attn_all

    def _L0_xattn_setup():
        import jax, jax.numpy as jnp
        import numpy as np
        D_MODEL = 128
        B, S = (4, 256)
        key = jax.random.key(seed)
        ks = jax.random.split(key, 10)
        s = 1.0 / np.sqrt(D_MODEL)
        return {'k': jax.random.normal(ks[0], (B, S, D_MODEL), jnp.float32), 'v': jax.random.normal(ks[1], (B, S, D_MODEL), jnp.float32), 'q': jax.random.normal(ks[2], (B, S, D_MODEL), jnp.float32), 'Wk': jax.random.normal(ks[3], (D_MODEL, D_MODEL), jnp.float32) * s, 'Wv': jax.random.normal(ks[4], (D_MODEL, D_MODEL), jnp.float32) * s, 'bv': jnp.zeros((D_MODEL,), jnp.float32), 'Wq': jax.random.normal(ks[5], (D_MODEL, D_MODEL), jnp.float32) * s, 'bq': jnp.zeros((D_MODEL,), jnp.float32), 'Wo': jax.random.normal(ks[6], (D_MODEL, D_MODEL), jnp.float32) * s, 'bo': jnp.zeros((D_MODEL,), jnp.float32)}
    _L0_xattn_all = _L0_xattn_setup()
    _L0_xattn_in = {k: v for k, v in _L0_xattn_all.items() if k in ('Wk', 'Wv', 'bv', 'Wq', 'bq', 'Wo', 'bo')}
    del _L0_xattn_all

    def _L0_ffn_setup():
        import jax, jax.numpy as jnp
        import numpy as np
        ALPHA = 1.5
        TEMP = 1.0
        N_ITER = 25
        THRESH = 1e-09

        def entmax_bisect(X, alpha=ALPHA, n_iter=N_ITER):
            d = X.shape[-1]
            inv_am1 = 1.0 / (alpha - 1.0)
            Xs = X * (alpha - 1.0)
            max_val = jnp.max(Xs, axis=-1, keepdims=True)
            tau_lo = max_val - 1.0
            tau_hi = max_val - (1.0 / d) ** (alpha - 1.0)
            f_lo = jnp.sum(jnp.maximum(Xs - tau_lo, 0.0) ** inv_am1, axis=-1, keepdims=True) - 1.0

            def body(i, carry):
                tau_lo, dm, _ = carry
                dm = dm * 0.5
                tau_m = tau_lo + dm
                f_m = jnp.sum(jnp.maximum(Xs - tau_m, 0.0) ** inv_am1, axis=-1, keepdims=True) - 1.0
                tau_lo = jnp.where(f_m * f_lo >= 0.0, tau_m, tau_lo)
                return (tau_lo, dm, tau_m)
            dm0 = tau_hi - tau_lo
            _, _, tau_m = jax.lax.fori_loop(0, n_iter, body, (tau_lo, dm0, tau_lo))
            p = jnp.maximum(Xs - tau_m, 0.0) ** inv_am1
            return p / jnp.sum(p, axis=-1, keepdims=True)
        key = jax.random.key(seed)
        ks = jax.random.split(key, 8)
        B, S, D, E = (2, 128, 128, 8)
        F = 4 * D
        return {'x': jax.random.normal(ks[0], (B, S, D), jnp.float32), 'Wr': jax.random.normal(ks[1], (D, E), jnp.float32) * 0.02, 'br': jnp.zeros((E,), jnp.float32), 'W1': jax.random.normal(ks[2], (E, D, F), jnp.float32) * 0.02, 'b1': jnp.zeros((E, F), jnp.float32), 'W2': jax.random.normal(ks[3], (E, F, D), jnp.float32) * 0.02, 'b2': jnp.zeros((E, D), jnp.float32)}
    _L0_ffn_all = _L0_ffn_setup()
    _L0_ffn_in = {k: v for k, v in _L0_ffn_all.items() if k in ('Wr', 'br', 'W1', 'b1', 'W2', 'b2')}
    del _L0_ffn_all
    return {'x': x, 'ctx_1024': ctx_1024, 'L0_attn_Wq': _L0_attn_in['Wq'], 'L0_attn_Wk': _L0_attn_in['Wk'], 'L0_attn_Wv': _L0_attn_in['Wv'], 'L0_attn_Wo': _L0_attn_in['Wo'], 'L0_attn_gamma': _L0_attn_in['gamma'], 'L0_attn_beta': _L0_attn_in['beta'], 'L0_xattn_Wk': _L0_xattn_in['Wk'], 'L0_xattn_Wv': _L0_xattn_in['Wv'], 'L0_xattn_bv': _L0_xattn_in['bv'], 'L0_xattn_Wq': _L0_xattn_in['Wq'], 'L0_xattn_bq': _L0_xattn_in['bq'], 'L0_xattn_Wo': _L0_xattn_in['Wo'], 'L0_xattn_bo': _L0_xattn_in['bo'], 'L0_ffn_Wr': _L0_ffn_in['Wr'], 'L0_ffn_br': _L0_ffn_in['br'], 'L0_ffn_W1': _L0_ffn_in['W1'], 'L0_ffn_b1': _L0_ffn_in['b1'], 'L0_ffn_W2': _L0_ffn_in['W2'], 'L0_ffn_b2': _L0_ffn_in['b2']}

def reference(x, ctx_1024, L0_attn_Wq, L0_attn_Wk, L0_attn_Wv, L0_attn_Wo, L0_attn_gamma, L0_attn_beta, L0_xattn_Wk, L0_xattn_Wv, L0_xattn_bv, L0_xattn_Wq, L0_xattn_bq, L0_xattn_Wo, L0_xattn_bo, L0_ffn_Wr, L0_ffn_br, L0_ffn_W1, L0_ffn_b1, L0_ffn_W2, L0_ffn_b2):
    import jax
    import jax.numpy as jnp

    def _L0_attn_ref(x, Wq, Wk, Wv, Wo, gamma, beta):
        import jax, jax.numpy as jnp
        import numpy as np
        NUM_HEADS = 16
        LN_EPS = 1e-05
        B, S, E = x.shape
        H = NUM_HEADS
        D = E // H
        scale = 1.0 / D ** 0.5
        q = x @ Wq.T
        k = x @ Wk.T * scale
        v = x @ Wv.T
        qh = q.reshape(B, S, H, D)
        kh = k.reshape(B, S, H, D)
        qk = jnp.einsum('bthd,bshd->bhts', qh, kh)
        causal = jnp.tril(jnp.ones((S, S), dtype=bool))
        qk = jnp.where(causal, qk, -jnp.inf)
        attn = jax.nn.softmax(qk, axis=-1)
        vh = v.reshape(B, S, D, H)
        qkv = jnp.einsum('bsdh,bhts->bthd', vh, attn)
        qkv = qkv.reshape(B, S, E)
        mu = jnp.mean(qkv, axis=-1, keepdims=True)
        var = jnp.mean(jnp.square(qkv - mu), axis=-1, keepdims=True)
        ln = (qkv - mu) * jax.lax.rsqrt(var + LN_EPS) * gamma + beta
        return ln @ Wo.T

    def _L0_xattn_ref(k, v, q, Wk, Wv, bv, Wq, bq, Wo, bo):
        import jax, jax.numpy as jnp
        import numpy as np
        D_MODEL = 128
        B, S = (4, 256)
        kp = jnp.einsum('bsd,ed->bse', k, Wk)
        vp = jnp.einsum('bsd,ed->bse', v, Wv) + bv
        qp = jnp.einsum('bsd,ed->bse', q, Wq) + bq
        scale = 1.0 / jnp.sqrt(jnp.float32(kp.shape[-1]))
        scores = jnp.einsum('bqd,bkd->bqk', qp, kp) * scale
        probs = jax.nn.softmax(scores, axis=-1)
        ctx = jnp.einsum('bqk,bkd->bqd', probs, vp)
        return jnp.einsum('bqd,ed->bqe', ctx, Wo) + bo

    def _L0_ffn_ref(x, Wr, br, W1, b1, W2, b2):
        import jax, jax.numpy as jnp
        import numpy as np
        ALPHA = 1.5
        TEMP = 1.0
        N_ITER = 25
        THRESH = 1e-09

        def entmax_bisect(X, alpha=ALPHA, n_iter=N_ITER):
            d = X.shape[-1]
            inv_am1 = 1.0 / (alpha - 1.0)
            Xs = X * (alpha - 1.0)
            max_val = jnp.max(Xs, axis=-1, keepdims=True)
            tau_lo = max_val - 1.0
            tau_hi = max_val - (1.0 / d) ** (alpha - 1.0)
            f_lo = jnp.sum(jnp.maximum(Xs - tau_lo, 0.0) ** inv_am1, axis=-1, keepdims=True) - 1.0

            def body(i, carry):
                tau_lo, dm, _ = carry
                dm = dm * 0.5
                tau_m = tau_lo + dm
                f_m = jnp.sum(jnp.maximum(Xs - tau_m, 0.0) ** inv_am1, axis=-1, keepdims=True) - 1.0
                tau_lo = jnp.where(f_m * f_lo >= 0.0, tau_m, tau_lo)
                return (tau_lo, dm, tau_m)
            dm0 = tau_hi - tau_lo
            _, _, tau_m = jax.lax.fori_loop(0, n_iter, body, (tau_lo, dm0, tau_lo))
            p = jnp.maximum(Xs - tau_m, 0.0) ** inv_am1
            return p / jnp.sum(p, axis=-1, keepdims=True)
        B, S, D = x.shape
        xt = x.reshape(B * S, D)
        logits = (xt @ Wr + br) / TEMP
        gates = entmax_bisect(logits)
        gates = jnp.where(gates > THRESH, gates, 0.0)
        h = jax.nn.relu(jnp.einsum('td,edf->etf', xt, W1) + b1[:, None, :])
        y = jnp.einsum('etf,efd->etd', h, W2) + b2[:, None, :]
        out = jnp.einsum('etd,te->td', y, gates)
        return out.reshape(B, S, D)
    x = x + _L0_attn_ref(_layernorm(x, axis=-1), L0_attn_Wq, L0_attn_Wk, L0_attn_Wv, L0_attn_Wo, L0_attn_gamma, L0_attn_beta)
    x = x + _L0_xattn_ref(ctx_1024, ctx_1024, _layernorm(x, axis=-1), L0_xattn_Wk, L0_xattn_Wv, L0_xattn_bv, L0_xattn_Wq, L0_xattn_bq, L0_xattn_Wo, L0_xattn_bo)
    x = x + _L0_ffn_ref(_layernorm(x, axis=-1), L0_ffn_Wr, L0_ffn_br, L0_ffn_W1, L0_ffn_b1, L0_ffn_W2, L0_ffn_b2)
    return x

_drawn_inputs = setup_inputs


def setup_inputs(seed=0):
    import zlib

    import numpy as np

    out = dict(_drawn_inputs(seed))
    spreads = {'L0_attn_gamma': (1.0, 0.2),
     'L0_attn_beta': (0.0, 0.1),
     'L0_xattn_bv': (0.0, 0.1),
     'L0_xattn_bq': (0.0, 0.445),
     'L0_xattn_bo': (0.0, 0.1),
     'L0_ffn_br': (0.0, 0.676),
     'L0_ffn_b1': (0.0, 0.8),
     'L0_ffn_b2': (0.0, 0.326)}
    factors = {'L0_ffn_Wr': 3.372, 'L0_ffn_W1': 3.408, 'L0_ffn_W2': 2.718}
    for name, (base, spread) in spreads.items():
        noise = np.random.default_rng([zlib.crc32(name.encode()), seed]).standard_normal(out[name].shape)
        drawn = base * np.exp(spread * noise) if base else spread * noise
        out[name] = jnp.asarray(drawn.astype(out[name].dtype))
    for name, factor in factors.items():
        out[name] = (out[name] * factor).astype(out[name].dtype)
    return out
```

```python
import concourse.bass as bass
from concourse import mybir
from contextlib import ExitStack

F32 = mybir.dt.float32
F32R = mybir.dt.float32r
BF16 = mybir.dt.bfloat16
ALU = mybir.AluOpType
ACT = mybir.ActivationFunctionType
AX = mybir.AxisListType

P = 128
B, S, E = 16, 256, 128
C = 64
H, D = 16, 8
NE, F = 8, 512
FB = F // P
TOK = 2 * S
NT = TOK // P
NP = B * S // TOK
NG, NJ = 4, 4
ROWS = 4 * D
VW = 32
LN_EPS = 1e-5
K_SCALE = float(D) ** -0.5
C_SCALE = float(E) ** -0.5
MASKED = -1e30
BISECTIONS = 25
WIDTH = 1.0 - (1.0 / NE) ** 0.5
CHUNKS = NE * FB
LAG = 2
SLOTS = CHUNKS + LAG + 1

A_STEPS = [
    (1, "T1", 0, "s"), (2, "Q", 0, "m"), (3, "K", 0, "s"), (4, "V", 0, "m"),
    *[(6 + n, "MAX", n, "s") for n in range(6)],
    (10, "MT", 0, "m"), (13, "MT", 1, "m"),
    *[(13 + n, "SC", n, "s") for n in range(8)],
    *[(15 + n, "PV", n, "m") for n in range(8)],
    (20, "BT", 0, "m"), (21, "BT", 1, "m"), (23, "BT", 2, "m"), (24, "BT", 3, "m"),
    (26, "TA", 0, "m"), (27, "WO", 0, "m"), (29, "T2", 0, "m"), (30, "XS", 0, "m"),
    (31, "PT", 0, "m"), (32, "XO", 0, "m"), (34, "T3", 0, "m"),
]
X_STEPS = [(0, "LG", 0, "s")] + [(t, "GA", e, "s") for e, t in enumerate((22, 23, 24, 25, 26, 28, 31, 34))]


def steps_of(slot, with_x, with_a):
    x = [s for s in X_STEPS if with_x and s[0] == slot]
    a = [s for s in sorted(A_STEPS, key=lambda s: s[0]) if with_a and s[0] == slot]
    return x + a


def fills(buffer, with_x, with_a):
    return [s[1:3] for t in range(SLOTS) for s in steps_of(t, with_x, with_a) if s[3] == buffer]


class Phase:

    def __init__(self, f, a):
        self.f, self.a = f, a
        self.with_x, self.with_a = f is not None, a is not None
        self.order = {b: fills(b, self.with_x, self.with_a) for b in "sm"}
        self.before = {}
        for b in "sm":
            first, loop = len(fills(b, False, True)), len(fills(b, True, True))
            self.before[b] = 0 if f is None else f * loop + first

    def fill(self, step):
        return self.before[step[3]] + self.order[step[3]].index(step[1:3])

    def slots(self):
        return range(SLOTS)

    def steps(self, slot):
        return steps_of(slot, self.with_x, self.with_a)


def run_phases(eng, body):
    body(Phase(None, 0))
    with eng.Fori(0, NP - 1) as i:
        body(Phase(i, i + 1))
    body(Phase(NP - 1, None))


def bass_decoder_layer(nc, x, ctx_in, wq, wk, wv, wo, gamma, beta, xwk, xwv, xbv, xwq, xbq, xwo, xbo,
                       wr, br, w1, b1, w2, b2, out):
    x_v = x.rearrange("b (t p) e -> p (b t) e", p=P)
    out_v = out.rearrange("b (t p) e -> p (b t) e", p=P)
    ctx_v = ctx_in.rearrange("(n b) c e -> (b c) n e", b=2)

    ctx = ExitStack()
    with ctx:
        def sb(name, shape, dt=F32):
            return ctx.enter_context(nc.sbuf_tensor(name, shape, dt))

        def ps(name, shape):
            return ctx.enter_context(nc.psum_tensor(name, shape, F32))

        def sem(name):
            return ctx.enter_context(nc.semaphore(name))

        ident = sb("ident", [P, P])
        ident_bf = sb("ident_bf", [P, P], BF16)
        causal = sb("causal", [P, NG, P], BF16)
        causal2 = sb("causal2", [P, 2, 2, P], BF16)
        zeros = sb("zeros", [NJ, 1, TOK])
        ones_r = sb("ones_r", [2, P], F32R)
        WNAMES = ["wq", "wk", "wv", "wo", "xwk", "xwv", "xwo"]
        wT_hi = sb("wT_hi", [P, 7, P], F32R)
        wT_lo = sb("wT_lo", [P, 7, P], F32R)
        xwq_hi = sb("xwq_hi", [P, P], F32R)
        xwq_lo = sb("xwq_lo", [P, P], F32R)
        vec_rows = sb("vec_rows", [4, P])
        vec = sb("vec", [P, 4])
        bq_hi = sb("bq_hi", [P, 2], F32R)
        bq_lo = sb("bq_lo", [P, 2], F32R)
        xbo_b = sb("xbo_b", [P, P])
        br_b = sb("br_b", [P, NE])
        wr_in = sb("wr_in", [P, NE])
        wr_hi = sb("wr_hi", [P, NE], F32R)
        wr_lo = sb("wr_lo", [P, NE], F32R)
        bias_rows = sb("bias_rows", [CHUNKS + NE, P])
        biasT = sb("biasT", [P, CHUNKS + NE])
        w1_hi = sb("w1_hi", [P, NE, F], F32R)
        w1_lo = sb("w1_lo", [P, NE, F], F32R)
        w2_hi = sb("w2_hi", [P, CHUNKS, E], F32R)
        w2_lo = sb("w2_lo", [P, CHUNKS, E], F32R)
        ka_hi = sb("ka_hi", [P, NP * P], F32R)
        ka_lo = sb("ka_lo", [P, NP * P], F32R)
        kc = sb("kc", [2, NP * P], F32R)
        vo_hi = sb("vo_hi", [P, NP, E], F32R)
        vo_lo = sb("vo_lo", [P, NP, E], F32R)
        x_t = sb("x_t", [P, NT, E])
        st6 = sb("st6", [P, NT, 6])
        mv = sb("mv", [P, NT, 2])
        eps_t = sb("eps_t", [P, NT])
        minus_half = sb("minus_half", [P, NT])
        vareps = sb("vareps", [P, NT])
        rstd = sb("rstd", [P, NT])
        ln = sb("ln", [P, NT, E])
        tT_hi = sb("tT_hi", [P, TOK], F32R)
        tT_lo = sb("tT_lo", [P, TOK], F32R)
        q_hi = sb("q_hi", [P, TOK], F32R)
        q_lo = sb("q_lo", [P, TOK], F32R)
        k_hi = sb("k_hi", [P, TOK], F32R)
        k_lo = sb("k_lo", [P, TOK], F32R)
        qs = sb("qs", [P, NG, TOK], F32R)
        ks = sb("ks", [P, NG, TOK], F32R)
        v_t = sb("v_t", [P, NT, H, VW])
        negmax = sb("negmax", [P, NT, H])
        nm_hi, nm_lo = q_hi[0:H, :], q_lo[0:H, :]
        prob = sb("prob", [P, 2, NJ, 3 * P])
        aT = prob[:, 0, :, :].rearrange("p j s -> p (j s)")[:, 0:TOK]
        attT = sb("attT", [P, 2, NG, S])
        w_in = attT[:, :, :, :].rearrange("p b g s -> p (b g s)")[:, 0:8 * P].rearrange(
            "p (n e) -> p n e", e=P)
        rden = sb("rden", [P, H])
        kc_lo = k_lo[0:1, :]
        att = sb("att", [P, NT, E])
        x1 = sb("x1", [P, NT, E])
        x1b = att
        cmax = sb("cmax", [P, NT])
        csum = sb("csum", [P, NT])
        crec = sb("crec", [P, NT])
        cp = sb("cp", [P, NT, P])
        cpT_hi, cpT_lo = tT_hi, tT_lo
        x2 = sb("x2", [P, NT, E])
        fT_hi = sb("fT_hi", [P, TOK], F32R)
        fT_lo = sb("fT_lo", [P, TOK], F32R)
        hr = sb("hr", [P, 2, TOK])
        h_hi = sb("h_hi", [P, 3, TOK], F32R)
        h_lo = sb("h_lo", [P, 3, TOK], F32R)
        y_sb = sb("y_sb", [P, NE, TOK])
        stage = y_sb
        c_in = hr[:, :, :].rearrange("p b t -> p (b t)").rearrange("p (n e) -> p n e", e=E)
        (cT_hi, kp_hi, vp_hi), (cT_lo, kp_lo, vp_lo) = ([w[:, k, :] for k in range(3)] for w in (h_hi, h_lo))
        acc = sb("acc", [P, NT, E])
        lgt = sb("lgt", [P, NT, NE])
        lmax = sb("lmax", [P, NT])
        above = sb("above", [P, NT, NE])
        part = sb("part", [P, NT, NE])
        part2 = sb("part2", [P, NT, NE])
        mass = sb("mass", [P, NT])
        shift = sb("shift", [P, NT])
        gate0 = sb("gate0", [P, NT, NE])
        gate = sb("gate", [P, NT, NE])

        sbuf_s = ps("sbuf_s", [P, NJ, TOK])
        sbuf_m = ps("sbuf_m", [P, TOK])
        h_ps = ps("h_ps", [P, 2, TOK])
        y_ps = ps("y_ps", [P, TOK])
        ps_of = {"s": sbuf_s[:, 0, :], "m": sbuf_m[:, :]}

        w_loaded = sem("w_loaded")
        c_loaded = sem("c_loaded")
        w1_loaded = sem("w1_loaded")
        w2_loaded = sem("w2_loaded")
        stage_free = sem("stage_free")
        const_made = sem("const_made")
        ident_made = sem("ident_made")
        setup_done = sem("setup_done")
        w_split = sem("w_split")
        pe_set = sem("pe_set")
        set_hi = sem("set_hi")
        set_free = sem("set_free")
        dve_step = sem("dve_step")
        full = {b: sem(f"full_{b}") for b in "sm"}
        free = {b: sem(f"free_{b}") for b in "sm"}
        x_loaded = sem("x_loaded")
        x_used = sem("x_used")
        var_made = sem("var_made")
        rstd_made = sem("rstd_made")
        vareps_made = sem("vareps_made")
        normed = sem("normed")
        hi_made = sem("hi_made")
        lo_made = sem("lo_made")
        affine = sem("affine")
        kc_placed = sem("kc_placed")
        kc_split = sem("kc_split")
        stacked = sem("stacked")
        nm_stacked = sem("nm_stacked")
        nm_cleared = sem("nm_cleared")
        nm_made = sem("nm_made")
        v_made = sem("v_made")
        max_made = sem("max_made")
        exp_made = sem("exp_made")
        mask_turn = sem("mask_turn")
        prob_made = sem("prob_made")
        attT_made = sem("attT_made")
        att_made = sem("att_made")
        cmax_made = sem("cmax_made")
        cp_made = sem("cp_made")
        x1b_made = sem("x1b_made")
        x1_made = sem("x1_made")
        h_full = sem("h_full")
        h_free = sem("h_free")
        hr_made = sem("hr_made")
        hhi_made = sem("hhi_made")
        hlo_made = sem("hlo_made")
        second_done = sem("second_done")
        y_free = sem("y_free")
        acc_made = sem("acc_made")
        stored = sem("stored")

        block = ctx.enter_context(nc.Block())

        def wait_fill(eng, ph, step):
            eng.wait_ge(full[step[3]], ph.fill(step) + 1)

        def blocks(ap, first):
            b = ap.rearrange("p (c t) -> p c t", t=P)
            return b[:, 0:3:2, :] if first else b[:, 1, :]

        def words(ap):
            return ap.bitcast(F32)

        SPLIT = {"T1": 0, "Q": 1, "K": 2, "TA": 3, "T2": 4, "PT": 5, "T3": 6}
        NSPLIT = len(SPLIT)
        SPLIT_BUF = {"T1": (tT_hi, tT_lo), "Q": (q_hi, q_lo), "K": (k_hi, k_lo), "TA": (tT_hi, tT_lo),
                     "T2": (tT_hi, tT_lo), "PT": (cpT_hi, cpT_lo), "T3": (fT_hi, fT_lo)}
        SPLIT_SCALE = {"K": K_SCALE}
        STACK_DMAS = 2 * 3 * NG

        SETUP = [("wT", n) for n in range(7)] + [("vec", 0), ("bias", 0)]
        for half in range(2):
            SETUP += [("cT", half), ("kp", half), ("vp", half), ("ka", half), ("kc", half), ("vo", half)]

        @block.sync
        def _(sp):
            for n, w in enumerate([wq, wk, wv, wo, xwk, xwv, xwo, xwq]):
                sp.dma_start(w_in[:, n, :], w).then_inc(w_loaded, 16)
            for n, v in enumerate([gamma, beta, xbv, xbq]):
                sp.dma_start(vec_rows[n:n + 1, :], v.rearrange("(a e) -> a e", a=1)).then_inc(w_loaded, 16)
            sp.dma_start(bias_rows[0:CHUNKS, :], b1.rearrange("n (c p) -> (n c) p", p=P)).then_inc(w_loaded, 16)
            sp.dma_start(bias_rows[CHUNKS:CHUNKS + NE, :], b2).then_inc(w_loaded, 16)
            sp.dma_start(wr_in[:, :], wr).then_inc(w_loaded, 16)
            sp.dma_start(xbo_b[:, :], xbo.rearrange("(a e) -> a e", a=1).to_broadcast([P, E])).then_inc(w_loaded, 16)
            sp.dma_start(br_b[:, :], br.rearrange("(a e) -> a e", a=1).to_broadcast([P, NE])).then_inc(w_loaded, 16)
            sp.dma_start(c_in[:, :, :], ctx_v).then_inc(c_loaded, 16)

            def stack_rows(ph, name, n):
                hi, lo = SPLIT_BUF[name]
                to, order = (qs, (hi, lo, hi)) if name == "Q" else (ks, (hi, hi, lo))
                sp.wait_ge(lo_made, ph.a * NSPLIT + SPLIT[name] + 1)
                for r, src in enumerate(order):
                    for g in range(NG):
                        dst = to[r:P:4, g, :]
                        sp.dma_start(words(dst), words(src[g * 32:(g + 1) * 32, :])).then_inc(stacked, 16)

            def nm_rows(ph, b):
                sp.wait_ge(nm_made, ph.a * 2 + b + 1)
                for r, src in enumerate((nm_hi, nm_lo)):
                    for g in range(NG):
                        dst = qs[3 + 4 * r:P:ROWS, g, b * S:(b + 1) * S]
                        sp.dma_start(words(dst), words(src[g * NJ:(g + 1) * NJ, b * S:(b + 1) * S])).then_inc(nm_stacked, 16)

            def load_x(pair, first=False):
                if not first:
                    sp.wait_ge(x_used, pair)
                sp.dma_start(x_t[:, :, :], x_v[:, bass.ts(pair, NT), :]).then_inc(x_loaded, 16)

            load_x(0, True)
            sp.wait_ge(const_made, 9)
            for half in range(2):
                sp.wait_ge(kc_split, half + 1)
                sp.dma_start(words(kc[1:2, half * TOK:(half + 1) * TOK]), words(kc_lo)).then_inc(kc_placed, 16)
            sp.dma_start(stage[:, :, :], w1.rearrange("n d f -> d n f")).then_inc(w1_loaded, 16)

            def body(ph):
                for t in ph.slots():
                    for s in ph.steps(t):
                        if s[1] in ("Q", "K"):
                            stack_rows(ph, s[1], s)
                        if s[1] == "MT":
                            nm_rows(ph, s[2])
                        if s[1:3] == ("SC", 7):
                            wait_fill(sp, ph, s)
                            for r in range(2):
                                sp.dma_start(words(qs[3 + 4 * r:P:ROWS, :, :]), zeros[:, :, :].to_broadcast([NJ, NG, TOK])).then_inc(nm_cleared, 16)
                        if s[1] == "GA" and s[2] == NE - 1:
                            sp.wait_ge(acc_made, ph.f + 1)
                            sp.dma_start(out_v[:, bass.ts(ph.f, NT), :], acc[:, :, :]).then_inc(stored, 16)
                        if s[1] == "T2" and isinstance(ph.a, int):
                            sp.wait_ge(stage_free, 2)
                            sp.dma_start(stage[:, :, :].rearrange("p n f -> p (n f)").rearrange(
                                "p (c d) -> p c d", d=E), w2.rearrange("n (c p) d -> p (n c) d", p=P)).then_inc(w2_loaded, 16)

            body(Phase(None, 0))
            with sp.Fori(0, NP - 1) as i:
                load_x(i + 1)
                body(Phase(i, i + 1))
            body(Phase(NP - 1, None))
            sp.wait_ge(nm_cleared, 32 * NP)
            sp.wait_ge(stored, 16 * NP + 16)

        @block.gpsimd
        def _(pool):
            pool.memset(ident[:, :], 0.0).then_inc(ident_made, 1)
            pool.wait_ge(ident_made, 1)
            pool.affine_select(out=ident[:, :], in_=ident[:, :], compare_op=ALU.not_equal, fill=1.0, base=0,
                               pattern=[[-1, P]], channel_multiplier=1).then_inc(ident_made, 1)
            pool.memset(eps_t[:, :], LN_EPS).then_inc(ident_made, 1)
            pool.memset(minus_half[:, :], -0.5).then_inc(ident_made, 1)
            pool.memset(causal[:, :, :], 0.0).then_inc(ident_made, 1)
            pool.memset(causal2[:, :, :, :], 0.0).then_inc(ident_made, 1)
            pool.memset(v_t[:, :, :, :], 0.0).then_inc(ident_made, 1)
            pool.wait_ge(ident_made, 7)
            pool.tensor_copy(ident_bf[:, :], ident[:, :]).then_inc(const_made, 1)
            pool.affine_select(out=causal[:, :, :], in_=causal[:, :, :], compare_op=ALU.is_ge, fill=MASKED, base=0,
                               pattern=[[0, NG], [-1, P]], channel_multiplier=1).then_inc(const_made, 1)
            pool.affine_select(out=causal2[:, :, 1, :], in_=causal2[:, :, 1, :], compare_op=ALU.is_ge, fill=MASKED,
                               base=0, pattern=[[0, 2], [-1, P]], channel_multiplier=1).then_inc(const_made, 1)
            pool.memset(v_t[:, :, :, D:D + 1], 1.0).then_inc(const_made, 1)
            pool.memset(cp[:, :, :], 0.0).then_inc(const_made, 1)
            pool.memset(words(ks[:, :, :]), 1.0).then_inc(const_made, 1)
            pool.memset(words(qs[:, :, :]), 0.0).then_inc(const_made, 1)
            pool.memset(zeros[:, :, :], 0.0).then_inc(const_made, 1)
            pool.memset(words(ones_r[:, :]), 1.0).then_inc(const_made, 1)

            def mask(ph, n):
                pool.wait_ge(exp_made, ph.a * 8 + n + 1)
                pool.sem_inc(mask_turn, 1)
                v = prob[:, n % 2, :, 0:2 * P]
                pool.affine_select(out=v, in_=v, compare_op=ALU.is_ge, fill=0.0, base=0,
                                   pattern=[[0, NJ], [0, 2], [1, P]], channel_multiplier=-1).then_inc(prob_made, 1)

            def inverse_deviation(ph, which):
                pool.wait_ge(var_made, ph.a * 4 * NT + NT * (which + 1))
                pool.tensor_tensor(vareps[:, :], mv[:, :, 1], eps_t[:, :], ALU.add).then_inc(vareps_made, 1)
                pool.wait_ge(vareps_made, ph.a * 4 + which + 1)
                pool.tensor_tensor(rstd[:, :], vareps[:, :], minus_half[:, :], ALU.pow).then_inc(rstd_made, 1)

            def bias_residual(ph):
                pool.wait_ge(x1_made, ph.a + 1)
                pool.tensor_tensor(x1b[:, :, :], x1[:, :, :], xbo_b[:, :].unsqueeze(1).to_broadcast([P, NT, E]),
                                   ALU.add).then_inc(x1b_made, 1)

            def body(ph):
                if ph.with_a:
                    inverse_deviation(ph, 0)
                for t in ph.slots():
                    for s in ph.steps(t):
                        if s[1] == "SC":
                            mask(ph, s[2])
                        if s[1:3] in (("BT", 3), ("WO", 0), ("XO", 0)):
                            inverse_deviation(ph, ("BT", "WO", "XO").index(s[1]) + 1)
                        if s[1] == "WO":
                            bias_residual(ph)

            run_phases(pool, body)

        @block.tensor
        def _(pe):
            def three(out_ap, w_hi, w_lo, m_hi, m_lo, start=True, stop=True):
                pe.matmul(out_ap, w_hi, m_lo, start=start, stop=False)
                pe.matmul(out_ap, w_lo, m_hi, start=False, stop=False)
                return pe.matmul(out_ap, w_hi, m_hi, start=False, stop=stop)

            pe.wait_ge(ident_made, 2)
            pe.wait_ge(w_loaded, 16 * 17)
            for n, (what, i) in enumerate(SETUP):
                if n >= 1:
                    pe.wait_ge(set_free, n)
                dst = sbuf_m if n % 2 else sbuf_s[:, 0, :]
                if what == "wT":
                    last = pe.transpose(dst[:, 0:P], w_in[:, i, :], ident[:, :])
                if what == "vec":
                    last = pe.transpose(dst[:, 0:4], vec_rows[:, :], ident[0:4, 0:4])
                if what == "bias":
                    last = pe.transpose(dst[:, 0:CHUNKS + NE], bias_rows[:, :], ident[0:CHUNKS + NE, 0:CHUNKS + NE])
                if what == "cT":
                    pe.wait_ge(c_loaded, 16)
                    for k in range(NT):
                        last = pe.transpose(dst[:, k * P:(k + 1) * P], c_in[:, i * NT + k, :], ident[:, :])
                if what == "kp":
                    last = three(dst[:, :], wT_hi[:, 4, :], wT_lo[:, 4, :], cT_hi[:, :], cT_lo[:, :])
                if what == "vp":
                    last = three(dst[:, :], wT_hi[:, 5, :], wT_lo[:, 5, :], cT_hi[:, :], cT_lo[:, :])
                if what == "ka":
                    last = three(dst[:, :], xwq_hi[:, :], xwq_lo[:, :], kp_hi[:, :], kp_lo[:, :])
                if what == "kc":
                    last = three(dst[0:2, :], bq_hi[:, :], bq_lo[:, :], kp_hi[:, :], kp_lo[:, :])
                if what == "vo":
                    for k in range(NT):
                        w = slice(k * P, (k + 1) * P)
                        last = three(dst[:, w], vp_hi[:, w], vp_lo[:, w], wT_hi[:, 6, :], wT_lo[:, 6, :])
                last.then_inc(pe_set, 1)
            pe.wait_ge(set_free, len(SETUP))
            pe.wait_ge(const_made, 9)
            pe.wait_ge(kc_placed, 32)

            def transposes(ph, dst, src):
                for k in range(NT):
                    last = pe.transpose(dst[:, k * P:(k + 1) * P], src[:, k, :], ident[:, :])
                return last

            def project_rows(dst, t_hi, t_lo, w_hi, w_lo):
                for k in range(NT):
                    w = slice(k * P, (k + 1) * P)
                    last = three(dst[:, w], t_hi[:, w], t_lo[:, w], w_hi, w_lo)
                return last

            def max_scores(ph, n):
                b, kind = divmod(n, 3)
                tile = 2 * b + (kind > 0)
                if n == 0:
                    pe.wait_ge(stacked, (ph.a + 1) * 16 * STACK_DMAS)
                    if ph.with_x:
                        pe.wait_ge(nm_cleared, ph.a * 32)
                for j in range(NJ):
                    m = causal[:, :, :] if kind == 0 else causal2[:, :, :, :]
                    pe.matmul(sbuf_s[:, j, :], ident_bf[:, :], m, start=True, stop=True)
                gs, width = (range(NG), P) if kind == 0 else (range(2 * kind - 2, 2 * kind), S)
                for at, g in enumerate(gs):
                    for j in range(NJ):
                        r = slice(32 * j, 32 * j + ROWS)
                        last = pe.matmul(sbuf_s[:, j, at * width:(at + 1) * width],
                                         qs[r, g, tile * P:(tile + 1) * P], ks[r, g, b * S:b * S + width],
                                         start=False, stop=True, skip_group_check=True)
                return last

            def scores(ph, n):
                b, g = divmod(n, NG)
                if g == 0:
                    pe.wait_ge(nm_stacked, ph.a * 256 + 128 * (b + 1))
                for first in (True, False):
                    for j in range(NJ):
                        r = slice(32 * j, 32 * j + ROWS)
                        k0, q0, w = (0, 0, S) if first else (P, P, P)
                        last = pe.matmul(blocks(sbuf_s[:, j, 0:3 * P], first), ks[r, g, b * S + k0:b * S + k0 + P],
                                         qs[r, g, b * S + q0:b * S + q0 + w], start=True, stop=True)
                return last

            def values(ph, n):
                b, g = divmod(n, NG)
                pe.wait_ge(prob_made, ph.a * 8 + n + 1)
                if n == 0:
                    pe.wait_ge(v_made, ph.a + 1)
                for first in (True, False):
                    for j in range(NJ):
                        o = sbuf_m[32 * j:32 * j + VW, :]
                        h = g * NJ + j
                        if first:
                            last = pe.matmul(o[:, 0:S], v_t[:, 2 * b, h, :], blocks(prob[:, n % 2, j, :], True), start=True, stop=True)
                        else:
                            last = pe.matmul(o[:, P:S], v_t[:, 2 * b + 1, h, :], blocks(prob[:, n % 2, j, :], False),
                                             start=False, stop=True, skip_group_check=True)
                return last

            def step(ph, s):
                t, name, n, buf = s
                before = ph.fill(s)
                if not (isinstance(before, int) and before == 0):
                    pe.wait_ge(free[buf], before)
                dst = ps_of[buf]
                if name in ("T1", "TA", "T2", "T3"):
                    pe.wait_ge(normed, ph.a * 4 + ("T1", "TA", "T2", "T3").index(name) + 1)
                    last = transposes(ph, dst, ln)
                if name in ("Q", "K", "V"):
                    pe.wait_ge(lo_made, ph.a * NSPLIT + SPLIT["T1"] + 1)
                    w = "QKV".index(name)
                    if name == "V":
                        last = project_rows(dst, tT_hi, tT_lo, wT_hi[:, w, :], wT_lo[:, w, :])
                    else:
                        last = three(dst, wT_hi[:, w, :], wT_lo[:, w, :], tT_hi[:, :], tT_lo[:, :])
                if name == "MAX":
                    last = max_scores(ph, n)
                if name == "MT":
                    pe.wait_ge(max_made, ph.a * 2 + n + 1)
                    for k in range(2):
                        last = pe.transpose(dst[0:H, (2 * n + k) * P:(2 * n + k + 1) * P], negmax[:, 2 * n + k, :],
                                            ident[:, :])
                if name == "SC":
                    last = scores(ph, n)
                if name == "PV":
                    last = values(ph, n)
                if name == "BT":
                    b, k = divmod(n, 2)
                    pe.wait_ge(attT_made, ph.a * 8 + 4 * (b + 1))
                    for g in range(NG):
                        last = pe.transpose(dst[:, g * P:(g + 1) * P], attT[:, b, g, k * P:(k + 1) * P], ident[:, :])
                if name == "WO":
                    pe.wait_ge(lo_made, ph.a * NSPLIT + SPLIT["TA"] + 1)
                    last = project_rows(dst, tT_hi, tT_lo, wT_hi[:, 3, :], wT_lo[:, 3, :])
                if name == "XS":
                    pe.wait_ge(lo_made, ph.a * NSPLIT + SPLIT["T2"] + 1)
                    for k in range(NT):
                        w = slice(k * P, (k + 1) * P)
                        c = bass.ds(ph.a * P + (k // 2) * C, C)
                        o = dst[:, k * C:(k + 1) * C]
                        three(o, tT_hi[:, w], tT_lo[:, w], ka_hi[:, c], ka_lo[:, c], stop=False)
                        last = pe.matmul(o, ones_r[:, :], kc[:, c], start=False, stop=True)
                if name == "PT":
                    pe.wait_ge(cp_made, ph.a * NT + NT)
                    last = transposes(ph, dst, cp)
                if name == "XO":
                    pe.wait_ge(lo_made, ph.a * NSPLIT + SPLIT["PT"] + 1)
                    for k in range(NT):
                        w = slice(k * P, (k + 1) * P)
                        v = bass.ds(ph.a, 1)
                        last = three(dst[:, w], cpT_hi[:, w], cpT_lo[:, w], vo_hi[:, v, :], vo_lo[:, v, :])
                if name == "LG":
                    pe.wait_ge(lo_made, ph.f * NSPLIT + NSPLIT)
                    for k in range(NT):
                        w = slice(k * P, (k + 1) * P)
                        last = three(dst[:, k * NE:(k + 1) * NE], fT_hi[:, w], fT_lo[:, w], wr_hi[:, :], wr_lo[:, :])
                if name == "GA":
                    pe.wait_ge(y_free, ph.f * NE + n + 1)
                    for k in range(NT):
                        last = pe.transpose(dst[:, k * P:(k + 1) * P], y_sb[:, n, k * P:(k + 1) * P], ident[:, :])
                last.then_inc(full[buf], 1)

            def first_product(ph, c):
                e, fb = divmod(c, FB)
                if c == 0:
                    pe.wait_ge(lo_made, ph.f * NSPLIT + NSPLIT)
                    pe.wait_ge(w_split, 4)
                if c >= 2:
                    pe.wait_ge(h_free, ph.f * CHUNKS + c - 1)
                w = slice(fb * P, (fb + 1) * P)
                three(h_ps[:, c % 2, :], w1_hi[:, e, w], w1_lo[:, e, w], fT_hi[:, :], fT_lo[:, :]).then_inc(h_full, 1)

            def second_product(ph, c):
                e, fb = divmod(c, FB)
                pe.wait_ge(hlo_made, ph.f * CHUNKS + c + 1)
                if fb == 0 and e > 0:
                    pe.wait_ge(y_free, ph.f * NE + e)
                three(y_ps[:, :], w2_hi[:, c, :], w2_lo[:, c, :], h_hi[:, c % 3, :], h_lo[:, c % 3, :],
                      start=(fb == 0), stop=(fb == FB - 1)).then_inc(second_done, 1)

            def body(ph):
                for t in ph.slots():
                    if ph.with_x and t < CHUNKS:
                        first_product(ph, t)
                    if ph.with_x and 0 <= t - LAG < CHUNKS:
                        second_product(ph, t - LAG)
                    for s in ph.steps(t):
                        step(ph, s)

            run_phases(pe, body)

        @block.scalar
        def _(act):
            act.wait_ge(ident_made, 2)
            act.wait_ge(w_loaded, 16 * 17)
            act.activation(xwq_hi[:, :], w_in[:, 7, :], ACT.Copy).then_inc(set_hi, 1)
            act.activation(wr_hi[:, :], wr_in[:, :], ACT.Copy).then_inc(set_hi, 1)
            HI = {"kp": kp_hi[:, :], "cT": cT_hi[:, :]}
            for n, (what, i) in enumerate(SETUP):
                act.wait_ge(pe_set, n + 1)
                src = sbuf_m if n % 2 else sbuf_s[:, 0, :]
                half = slice(i * TOK, (i + 1) * TOK)
                if what == "wT":
                    s_ap = src[:, 0:P]
                    if i == 2:
                        s_ap = s_ap.rearrange("p (d h) -> p h d", h=H)
                        ins = act.activation(wT_hi[:, i, :].rearrange("p (h d) -> p h d", d=D), s_ap, ACT.Copy)
                    else:
                        ins = act.activation(wT_hi[:, i, :], s_ap, ACT.Copy)
                if what == "vec":
                    ins = act.activation(vec[:, :], src[:, 0:4], ACT.Copy)
                if what == "bias":
                    ins = act.activation(biasT[:, :], src[:, 0:CHUNKS + NE], ACT.Copy)
                if what in HI:
                    ins = act.activation(HI[what], src[:, :], ACT.Copy)
                if what == "vp":
                    act.wait_ge(set_hi, 10)
                    ins = act.activation(vp_hi[:, :], src[:, :], ACT.Identity, bias=vec[:, 2:3])
                if what == "ka":
                    ins = act.activation(ka_hi[:, half], src[:, :], ACT.Copy, scale=C_SCALE)
                if what == "kc":
                    ins = act.activation(kc[0:1, half], src[0:1, :], ACT.Copy, scale=C_SCALE)
                if what == "vo":
                    ins = act.activation(vo_hi[:, i * NT:(i + 1) * NT, :],
                                         src[:, :].rearrange("p (n e) -> p n e", e=E), ACT.Copy)
                ins.then_inc(set_hi, 1)
            act.wait_ge(w1_loaded, 16)
            act.activation(w1_hi[:, :, :], stage[:, :, :], ACT.Copy).then_inc(stage_free, 1)

            def split_hi(ph, s):
                wait_fill(act, ph, s)
                hi, _ = SPLIT_BUF[s[1]]
                if s[1] in ("Q", "K") and not isinstance(ph.a, int):
                    act.wait_ge(stacked, ph.a * 16 * STACK_DMAS)
                act.activation(hi[:, :], ps_of[s[3]], ACT.Copy, scale=SPLIT_SCALE.get(s[1], 1.0)).then_inc(hi_made, 1)

            def step(ph, s):
                t, name, n, buf = s
                if name in ("T1", "Q", "K", "T2", "PT", "T3"):
                    split_hi(ph, s)
                if name == "TA":
                    act.wait_ge(affine, ph.a + 1)
                    act.activation(tT_hi[:, :], aT[:, :], ACT.Copy).then_inc(hi_made, 1)
                if name == "SC":
                    wait_fill(act, ph, s)
                    if n >= 2:
                        act.wait_ge(full["m"], ph.fill((0, "PV", n - 2, "m")) + 1)
                    act.activation(prob[:, n % 2, :, :], sbuf_s[:, :, 0:3 * P], ACT.Exp).then_inc(exp_made, 1)
                if name == "PV":
                    wait_fill(act, ph, s)
                    act.activation(attT[:, n // NG, n % NG, :], sbuf_m[:, 0:S], ACT.Copy).then_inc(attT_made, 1)
                if name == "XS":
                    act.wait_ge(cmax_made, ph.a + 1)
                    for k in range(NT):
                        h0 = (k // 2) * C
                        act.activation(cp[:, k, h0:h0 + C], ps_of[buf][:, k * C:(k + 1) * C], ACT.Exp,
                                       bias=cmax[:, k:k + 1], accum_out=csum[:, k:k + 1]).then_inc(cp_made, 1)

            def hidden(ph, c):
                act.wait_ge(h_full, ph.f * CHUNKS + c + 1)
                if c >= 2:
                    act.wait_ge(hlo_made, ph.f * CHUNKS + c - 1)
                bias = biasT[:, c:c + 1]
                act.activation(hr[:, c % 2, :], h_ps[:, c % 2, :], ACT.Relu, bias=bias).then_inc(hr_made, 1)
                if c >= 3:
                    act.wait_ge(second_done, ph.f * CHUNKS + c - 2)
                act.activation(h_hi[:, c % 3, :], h_ps[:, c % 2, :], ACT.Relu, bias=bias).then_inc(h_free, 1)

            def evacuate_y(ph, e):
                act.wait_ge(second_done, ph.f * CHUNKS + FB * (e + 1))
                act.activation(y_sb[:, e, :], y_ps[:, :], ACT.Identity,
                               bias=biasT[:, CHUNKS + e:CHUNKS + e + 1]).then_inc(y_free, 1)

            def body(ph):
                for t in ph.slots():
                    if ph.with_x and t < CHUNKS:
                        hidden(ph, t)
                    c = t - LAG
                    if ph.with_x and 0 <= c < CHUNKS and c % FB == FB - 1:
                        evacuate_y(ph, c // FB)
                    for s in ph.steps(t):
                        step(ph, s)
                    if ph.f is None and t == 26:
                        act.wait_ge(w2_loaded, 16)
                        act.activation(w2_hi[:, :, :], stage[:, :, :].rearrange("p n f -> p (n f)").rearrange(
                            "p (c d) -> p c d", d=E), ACT.Copy).then_inc(stage_free, 1)

            run_phases(act, body)

        @block.vector
        def _(dve):
            steps_done = [0]

            def mark(ins):
                steps_done[0] += 1
                ins.then_inc(dve_step, 1)

            def settle():
                dve.wait_ge(dve_step, steps_done[0])

            dve.sem_inc(stored, 16)
            dve.wait_ge(set_hi, 2)
            dve.tensor_tensor(xwq_lo[:, :], w_in[:, 7, :], xwq_hi[:, :], ALU.subtract)
            dve.tensor_tensor(wr_lo[:, :], wr_in[:, :], wr_hi[:, :], ALU.subtract)
            for n, (what, i) in enumerate(SETUP):
                dve.wait_ge(set_hi, n + 3)
                src = sbuf_m if n % 2 else sbuf_s[:, 0, :]
                half = slice(i * TOK, (i + 1) * TOK)
                if what == "wT":
                    if i == 2:
                        ins = dve.tensor_tensor(wT_lo[:, i, :].rearrange("p (h d) -> p h d", d=D),
                                                src[:, 0:P].rearrange("p (d h) -> p h d", h=H),
                                                wT_hi[:, i, :].rearrange("p (h d) -> p h d", d=D), ALU.subtract)
                    else:
                        ins = dve.tensor_tensor(wT_lo[:, i, :], src[:, 0:P], wT_hi[:, i, :], ALU.subtract)
                if what == "vec":
                    mark(dve.tensor_copy(bq_hi[:, 0:1], vec[:, 3:4]))
                    mark(dve.tensor_copy(bq_hi[:, 1:2], vec[:, 3:4]))
                    settle()
                    dve.tensor_tensor(bq_lo[:, 0:1], vec[:, 3:4], bq_hi[:, 0:1], ALU.subtract)
                    ins = dve.tensor_tensor(bq_lo[:, 1:2], vec[:, 3:4], bq_hi[:, 0:1], ALU.subtract)
                if what == "bias":
                    dve.sem_inc(set_free, 1)
                    continue
                if what == "cT":
                    ins = dve.tensor_tensor(cT_lo[:, :], src[:, :], cT_hi[:, :], ALU.subtract)
                if what == "kp":
                    ins = dve.tensor_tensor(kp_lo[:, :], src[:, :], kp_hi[:, :], ALU.subtract)
                if what == "vp":
                    ins = dve.scalar_tensor_tensor(out=vp_lo[:, :], in0=src[:, :], scalar=vec[:, 2:3],
                                                   in1=vp_hi[:, :], op0=ALU.add, op1=ALU.subtract)
                if what == "ka":
                    ins = dve.scalar_tensor_tensor(out=ka_lo[:, half], in0=src[:, :], scalar=C_SCALE,
                                                   in1=ka_hi[:, half], op0=ALU.mult, op1=ALU.subtract)
                if what == "kc":
                    ins = dve.scalar_tensor_tensor(out=kc_lo[:, :], in0=src[0:1, :], scalar=C_SCALE,
                                                   in1=kc[0:1, half], op0=ALU.mult, op1=ALU.subtract)
                if what == "vo":
                    ins = dve.tensor_tensor(vo_lo[:, i * NT:(i + 1) * NT, :],
                                            src[:, :].rearrange("p (n e) -> p n e", e=E),
                                            vo_hi[:, i * NT:(i + 1) * NT, :], ALU.subtract)
                ins.then_inc(set_free, 1)
                if what == "kc":
                    dve.wait_ge(set_free, n + 1)
                    dve.sem_inc(kc_split, 1)
                    dve.wait_ge(kc_placed, 16 * (i + 1))

            def layer_norm(ph, which, src):
                if which:
                    settle()
                for k in range(NT):
                    mark(dve.bn_stats(st6[:, k, :], src[:, k, :]))
                settle()
                for k in range(NT):
                    dve.bn_aggr(mv[:, k, :], st6[:, k, :]).then_inc(var_made, 1)
                dve.wait_ge(rstd_made, ph.a * 4 + which + 1)
                for k in range(NT):
                    ins = dve.tensor_scalar(ln[:, k, :], src[:, k, :], mv[:, k, 0:1], rstd[:, k:k + 1],
                                            ALU.subtract, ALU.mult)
                ins.then_inc(normed, 1)

            def split_lo(ph, s):
                name, buf = s[1], s[3]
                hi, lo = SPLIT_BUF[name]
                dve.wait_ge(hi_made, ph.a * NSPLIT + SPLIT[name] + 1)
                src = ps_of[buf]
                if name in SPLIT_SCALE:
                    ins = dve.scalar_tensor_tensor(out=lo[:, :], in0=src, scalar=SPLIT_SCALE[name], in1=hi[:, :],
                                                   op0=ALU.mult, op1=ALU.subtract)
                elif name == "TA":
                    ins = dve.tensor_tensor(lo[:, :], aT[:, :], hi[:, :], ALU.subtract)
                else:
                    ins = dve.tensor_tensor(lo[:, :], src, hi[:, :], ALU.subtract)
                ins.then_inc(lo_made, 1)
                return ins

            def step(ph, s):
                t, name, n, buf = s
                src = ps_of[buf]
                if name in ("T1", "Q", "K", "T2", "PT", "T3"):
                    split_lo(ph, s)
                    dve.wait_ge(lo_made, ph.a * NSPLIT + SPLIT[name] + 1)
                    dve.sem_inc(free[buf], 1)
                if name == "V":
                    wait_fill(dve, ph, s)
                    dve.tensor_copy(v_t[:, :, :, 0:D], src.rearrange("p (k h d) -> p k h d", h=H, d=D)).then_inc(v_made, 1)
                    dve.wait_ge(v_made, ph.a + 1)
                    dve.sem_inc(free[buf], 1)
                if name == "MAX":
                    wait_fill(dve, ph, s)
                    b, kind = divmod(n, 3)
                    tile = 2 * b + (kind > 0)
                    if kind == 0:
                        o = negmax[:, tile, :].rearrange("p (g j) -> p j g", j=NJ)
                        i_ = sbuf_s[:, :, :].rearrange("p j (g s) -> p j g s", g=NG)
                    else:
                        o = negmax[:, tile, 8 * (kind - 1):8 * kind].rearrange("p (g j) -> p j g", j=NJ)
                        i_ = sbuf_s[:, :, :].rearrange("p j (g s) -> p j g s", g=2)
                    dve.tensor_reduce(o, i_, AX.X, ALU.max, negate=True).then_inc(free[buf], 1)
                    if kind == 2:
                        dve.wait_ge(free[buf], ph.fill(s) + 1)
                        dve.sem_inc(max_made, 1)
                if name == "MT":
                    wait_fill(dve, ph, s)
                    if not isinstance(ph.a, int) or n:
                        dve.wait_ge(nm_stacked, ph.a * 256 + 128 * n)
                    w = slice(n * S, (n + 1) * S)
                    mark(dve.tensor_copy(nm_hi[:, w], src[0:H, w]))
                    settle()
                    dve.tensor_tensor(nm_lo[:, w], src[0:H, w], nm_hi[:, w], ALU.subtract).then_inc(nm_made, 1)
                    dve.wait_ge(nm_made, ph.a * 2 + n + 1)
                    dve.sem_inc(free[buf], 1)
                if name == "SC":
                    dve.wait_ge(exp_made, ph.a * 8 + n + 1)
                    dve.sem_inc(free[buf], 1)
                if name == "PV":
                    dve.wait_ge(attT_made, ph.a * 8 + n + 1)
                    dve.sem_inc(free[buf], 1)
                if name == "BT":
                    wait_fill(dve, ph, s)
                    v = src.rearrange("p (h w) -> p h w", w=VW)
                    mark(dve.reciprocal(rden[:, :], v[:, :, D]))
                    settle()
                    ins = dve.tensor_tensor(att[:, n, :].rearrange("p (h d) -> p h d", d=D), v[:, :, 0:D],
                                            rden[:, :].unsqueeze(2).to_broadcast([P, H, D]), ALU.mult)
                    mark(ins)
                    settle()
                    dve.sem_inc(free[buf], 1)
                    if n == 3:
                        layer_norm(ph, 1, att)
                if name == "TA":
                    wait_fill(dve, ph, s)
                    dve.tensor_scalar(aT[:, :], src, vec[:, 0:1], vec[:, 1:2], ALU.mult, ALU.add).then_inc(affine, 1)
                    dve.wait_ge(affine, ph.a + 1)
                    dve.sem_inc(free[buf], 1)
                    split_lo(ph, s)
                if name == "WO":
                    wait_fill(dve, ph, s)
                    if not isinstance(ph.a, int):
                        dve.wait_ge(x1b_made, ph.a)
                    dve.tensor_tensor(x1[:, :, :], x_t[:, :, :], src.rearrange("p (k e) -> p k e", e=E),
                                      ALU.add).then_inc(x1_made, 1)
                    dve.wait_ge(x1_made, ph.a + 1)
                    dve.sem_inc(free[buf], 1)
                    dve.sem_inc(x_used, 1)
                    layer_norm(ph, 2, x1)
                if name == "XS":
                    wait_fill(dve, ph, s)
                    dve.tensor_reduce(cmax[:, :], src[:, 0:NT * C].rearrange("p (k c) -> p k c", c=C), AX.X,
                                      ALU.max, negate=True).then_inc(cmax_made, 1)
                    dve.wait_ge(cp_made, ph.a * NT + NT)
                    dve.sem_inc(free[buf], 1)
                    mark(dve.reciprocal(crec[:, :], csum[:, :]))
                    settle()
                if name == "XO":
                    wait_fill(dve, ph, s)
                    dve.wait_ge(x1b_made, ph.a + 1)
                    for k in range(NT):
                        mark(dve.scalar_tensor_tensor(out=x2[:, k, :], in0=src[:, k * E:(k + 1) * E],
                                                      scalar=crec[:, k:k + 1], in1=x1b[:, k, :],
                                                      op0=ALU.mult, op1=ALU.add))
                    settle()
                    dve.sem_inc(free[buf], 1)
                    layer_norm(ph, 3, x2)
                if name == "LG":
                    wait_fill(dve, ph, s)
                    mark(dve.tensor_tensor(lgt[:, :, :], src[:, 0:NT * NE].rearrange("p (k e) -> p k e", e=NE),
                                           br_b[:, :].unsqueeze(1).to_broadcast([P, NT, NE]), ALU.add))
                    settle()
                    dve.sem_inc(free[buf], 1)
                    mark(dve.tensor_scalar(part[:, :, :], lgt[:, :, :], 0.5, None, ALU.mult))
                    settle()
                    mark(dve.tensor_reduce(lmax[:, :], part[:, :, :], AX.X, ALU.max))
                    settle()
                    mark(dve.tensor_scalar(shift[:, :], lmax[:, :], -1.0, None, ALU.add))
                    settle()
                    mark(dve.tensor_tensor(above[:, :, :], part[:, :, :],
                                           shift[:, :].unsqueeze(2).to_broadcast([P, NT, NE]), ALU.subtract))
                if name == "GA":
                    wait_fill(dve, ph, s)
                    settle()
                    for k in range(NT):
                        mark(dve.scalar_tensor_tensor(out=acc[:, k, :], in0=src[:, k * E:(k + 1) * E],
                                                      scalar=gate[:, k, n:n + 1],
                                                      in1=(acc if n else x2)[:, k, :], op0=ALU.mult, op1=ALU.add))
                    settle()
                    dve.sem_inc(free[buf], 1)
                    if n == NE - 1:
                        dve.sem_inc(acc_made, 1)

            def bisect(it):
                width = WIDTH * 0.5 ** (it + 1)
                last = it == BISECTIONS - 1
                settle()
                mark(dve.tensor_scalar(part[:, :, :], above[:, :, :], width, 0.0, ALU.subtract, ALU.max))
                settle()
                mark(dve.tensor_tensor(part2[:, :, :], part[:, :, :], part[:, :, :], ALU.mult))
                settle()
                mark(dve.tensor_reduce(mass[:, :], part2[:, :, :], AX.X, ALU.add))
                if not last:
                    settle()
                    mark(dve.tensor_scalar(shift[:, :], mass[:, :], 1.0, width, ALU.is_ge, ALU.mult))
                    settle()
                    mark(dve.tensor_tensor(above[:, :, :], above[:, :, :],
                                           shift[:, :].unsqueeze(2).to_broadcast([P, NT, NE]), ALU.subtract))

            def gates():
                settle()
                mark(dve.reciprocal(shift[:, :], mass[:, :]))
                settle()
                mark(dve.tensor_tensor(gate0[:, :, :], part2[:, :, :],
                                       shift[:, :].unsqueeze(2).to_broadcast([P, NT, NE]), ALU.mult))
                settle()
                mark(dve.scalar_tensor_tensor(out=gate[:, :, :], in0=gate0[:, :, :], scalar=1e-9,
                                              in1=gate0[:, :, :], op0=ALU.is_gt, op1=ALU.mult))

            def hidden_lo(ph, c):
                dve.wait_ge(h_free, ph.f * CHUNKS + c + 1)
                dve.tensor_tensor(h_lo[:, c % 3, :], hr[:, c % 2, :], h_hi[:, c % 3, :], ALU.subtract)\
                   .then_inc(hlo_made, 1)

            def body(ph):
                if ph.with_a:
                    dve.wait_ge(x_loaded, ph.a * 16 + 16)
                    layer_norm(ph, 0, x_t)
                for t in ph.slots():
                    if ph.with_x and t < CHUNKS:
                        hidden_lo(ph, t)
                    for s in ph.steps(t):
                        step(ph, s)
                    if ph.with_x and 1 <= t <= 13:
                        for it in (2 * t - 2, 2 * t - 1):
                            if it < BISECTIONS:
                                bisect(it)
                    if ph.with_x and t == 14:
                        gates()
                        dve.wait_ge(stored, ph.f * 16 + 16)
                    if ph.f is None and t == 4:
                        dve.wait_ge(stage_free, 1)
                        dve.tensor_tensor(w1_lo[:, :, :], stage[:, :, :], w1_hi[:, :, :], ALU.subtract)\
                           .then_inc(stage_free, 1)
                    if ph.f is None and t == 27:
                        dve.wait_ge(stage_free, 3)
                        dve.tensor_tensor(w2_lo[:, :, :], stage[:, :, :].rearrange("p n f -> p (n f)").rearrange(
                            "p (c d) -> p c d", d=E), w2_hi[:, :, :], ALU.subtract).then_inc(w_split, 4)
                settle()
                dve.sem_clear(dve_step)
                steps_done[0] = 0

            run_phases(dve, body)


_INS = ["x", "ctx_1024", "L0_attn_Wq", "L0_attn_Wk", "L0_attn_Wv", "L0_attn_Wo", "L0_attn_gamma", "L0_attn_beta",
        "L0_xattn_Wk", "L0_xattn_Wv", "L0_xattn_bv", "L0_xattn_Wq", "L0_xattn_bq", "L0_xattn_Wo", "L0_xattn_bo",
        "L0_ffn_Wr", "L0_ffn_br", "L0_ffn_W1", "L0_ffn_b1", "L0_ffn_W2", "L0_ffn_b2"]
_OUTS = [((B, S, E), "float32")]


def kernel(**inputs):
    import numpy as _np
    import concourse.bacc as _bacc
    from concourse import mybir as _mybir
    from concourse.bass_utils import run_bass_kernel_spmd as _run

    nc = _bacc.Bacc("TRN2", target_bir_lowering=False, num_devices=1)
    arrays, args = {}, []
    for name in _INS:
        a = _np.ascontiguousarray(inputs[name])
        arrays[f"in_{name}_dram"] = a
        args.append(nc.dram_tensor(f"in_{name}_dram", a.shape, _mybir.dt.from_np(a.dtype), kind="ExternalInput").ap())
    for i, (shape, dtype) in enumerate(_OUTS):
        dt = _mybir.dt.from_np(_np.dtype(dtype))
        args.append(nc.dram_tensor(f"out_{i}_dram", shape, dt, kind="ExternalOutput").ap())
    bass_decoder_layer(nc, *args)
    r = _run(nc, [arrays], core_ids=[0])
    return r.results[0]["out_0_dram"]
```

```python
import concourse.bass as bass
from concourse import mybir
from contextlib import ExitStack

F32 = mybir.dt.float32
F32R = mybir.dt.float32r
BF16 = mybir.dt.bfloat16
ALU = mybir.AluOpType
ACT = mybir.ActivationFunctionType
AX = mybir.AxisListType

P = 128
B, S, E = 16, 256, 128
C = 64
H, D = 16, 8
NE, F = 8, 512
FB = F // P
TOK = 2 * S
NT = TOK // P
NP = B * S // TOK
NG, NJ = 4, 4
ROWS = 4 * D
VW = 32
LN_EPS = 1e-5
K_SCALE = float(D) ** -0.5
C_SCALE = float(E) ** -0.5
MASKED = -1e30
BISECTIONS = 25
WIDTH = 1.0 - (1.0 / NE) ** 0.5
CHUNKS = NE * FB
DVE_BLOCKS = 12
LAG = 2
SLOTS = CHUNKS + LAG + 2

LN_Z = 1
Z_STEPS = [
    (4, "T1", 0, "m"), (6, "Q", 0, "m"), (7, "K", 0, "m"), (11, "V", 0, "m"),
    *[(16 + n, "MAX", n, "st"[n % 2]) for n in range(12)],
    (23, "MT", 0, "m"), (29, "MT", 1, "m"),
]
A_STEPS = [
    *[(n // 2, "SC", n, "st"[n % 2]) for n in range(16)],
    *[(n + 2, "PV", n, "m") for n in range(8)],
    (7, "BT", 0, "m"), (8, "BT", 1, "m"), (10, "BT", 2, "m"), (11, "BT", 3, "m"),
    (15, "TA", 0, "m"), (17, "WO", 0, "m"), (21, "T2", 0, "m"), (23, "XS", 0, "m"),
    (25, "PT", 0, "m"), (27, "XO", 0, "m"), (31, "T3", 0, "m"),
]
X_STEPS = [(0, "LG", 0, "m")] + [(t, "GA", n, "st"[n % 2]) for n, t in enumerate((29, 31, 33, 35))]
BISECT_FROM = 1
W_STEPS = [(8, "wo", 0, "u"), (8, "xwk", 0, "v"), (9, "xwv", 0, "y"), (9, "xwo", 0, "u"), (9, "bias", 0, "v"),
           (10, "cT", 0, "y"), (11, "kp", 0, "u"), (12, "vp", 0, "v"), (13, "ka", 0, "y"), (13, "kc", 0, "u"),
           (14, "vo", 0, "v"), (14, "cT", 1, "y"), (16, "kp", 1, "u"), (17, "vp", 1, "v"), (18, "ka", 1, "y"),
           (19, "kc", 1, "u"), (20, "vo", 1, "v")]
SPREAD = {**{(name, 0): b for name, b in (("T1", "u"), ("Q", "v"), ("K", "y"), ("V", "u"))},
          **{("PV", n): "mu"[n % 2] for n in range(8)}, **{("BT", n): "vy"[n % 2] for n in range(4)}}
W_ORDER = [s[1:3] for s in sorted(W_STEPS, key=lambda s: s[0])]


BUFFERS = "stmuvy"


class Phase:

    KINDS = [("Z", "W"), ("A", "Z"), ("X", "A", "Z"), ("X", "A"), ("X",)]

    def __init__(self, kind, f=None, a=None, z=None):
        self.f, self.a, self.z = f, a, z
        self.parts = self.KINDS[kind]
        self.once = kind < 2
        before = lambda b: sum(self.count(k, b) for k in range(min(kind, 2)))
        rounds = 0 if kind < 2 else f if kind == 2 else NP - 2
        self.before = {b: before(b) + (rounds * self.count(2, b) if self.count(2, b) else 0)
                       + (self.count(3, b) if kind == 4 else 0) for b in BUFFERS}
        self.order = {b: [s[1:3] for s in self.all_steps(self.parts) if s[3] == b] for b in BUFFERS}

    @staticmethod
    def all_steps(parts):
        lists = {"X": X_STEPS, "A": A_STEPS, "Z": Z_STEPS, "W": W_STEPS}
        steps = sorted((s for p in "XAZW" if p in parts for s in lists[p]), key=lambda s: s[0])
        return steps if "X" in parts else [(*s[:3], SPREAD.get(s[1:3], s[3])) for s in steps]

    @classmethod
    def count(cls, kind, b):
        return sum(s[3] == b for s in cls.all_steps(cls.KINDS[kind]))

    def fill(self, step):
        return self.before[step[3]] + self.order[step[3]].index(step[1:3])

    def find(self, name, n=0):
        return next(s for s in self.all_steps(self.parts) if s[1:3] == (name, n))

    def steps(self, slot):
        return [s for s in self.all_steps(self.parts) if s[0] == slot]


def run_phases(eng, body):
    body(Phase(0, z=0))
    body(Phase(1, a=0, z=1))
    with eng.Fori(0, NP - 2) as i:
        body(Phase(2, f=i, a=i + 1, z=i + 2))
    body(Phase(3, f=NP - 2, a=NP - 1))
    body(Phase(4, f=NP - 1))


def bass_decoder_layer(nc, x, ctx_in, wq, wk, wv, wo, gamma, beta, xwk, xwv, xbv, xwq, xbq, xwo, xbo,
                       wr, br, w1, b1, w2, b2, out):
    x_v = x.rearrange("b (t p) e -> p (b t) e", p=P)
    out_v = out.rearrange("b (t p) e -> p (b t) e", p=P)
    ctx_v = ctx_in.rearrange("(n b) c e -> (b c) n e", b=2)

    ctx = ExitStack()
    with ctx:
        def sb(name, shape, dt=F32):
            return ctx.enter_context(nc.sbuf_tensor(name, shape, dt))

        def ps(name, shape):
            return ctx.enter_context(nc.psum_tensor(name, shape, F32))

        def sem(name):
            return ctx.enter_context(nc.semaphore(name))

        ident = sb("ident", [P, P])
        ident_bf = sb("ident_bf", [P, P], BF16)
        causal = sb("causal", [P, NG, P], BF16)
        zeros = sb("zeros", [NJ, 1, TOK])
        ones_r = sb("ones_r", [2, P], F32R)
        wT_hi = sb("wT_hi", [P, 4, P], F32R)
        wT_lo = sb("wT_lo", [P, 4, P], F32R)
        xwq_hi = sb("xwq_hi", [P, P], F32R)
        xwq_lo = sb("xwq_lo", [P, P], F32R)
        vec_rows = sb("vec_rows", [4, P])
        vec = sb("vec", [P, 4])
        bq_hi = sb("bq_hi", [P, 2], F32R)
        bq_lo = sb("bq_lo", [P, 2], F32R)
        xbo_b = sb("xbo_b", [P, P])
        br_b = sb("br_b", [P, NE])
        wr_in = sb("wr_in", [P, NE])
        wr_hi = sb("wr_hi", [P, NE], F32R)
        wr_lo = sb("wr_lo", [P, NE], F32R)
        bias_rows = sb("bias_rows", [CHUNKS + NE, P])
        biasT = sb("biasT", [P, CHUNKS + NE])
        w1_hi = sb("w1_hi", [P, NE, F], F32R)
        w1_lo = sb("w1_lo", [P, NE, F], F32R)
        w2_hi = sb("w2_hi", [P, CHUNKS, E], F32R)
        w2_lo = sb("w2_lo", [P, CHUNKS, E], F32R)
        ka_hi = sb("ka_hi", [P, NP * P], F32R)
        ka_lo = sb("ka_lo", [P, NP * P], F32R)
        kc = sb("kc", [2, NP * P], F32R)
        vo_hi = sb("vo_hi", [P, NP, E], F32R)
        vo_lo = sb("vo_lo", [P, NP, E], F32R)
        x_t = sb("x_t", [P, NT, E])
        x_r = sb("x_r", [P, NT, E])
        st6 = sb("st6", [P, NT, 6])
        mv = sb("mv", [P, NT, 2])
        eps_t = sb("eps_t", [P, NT])
        minus_half = sb("minus_half", [P, NT])
        vareps = sb("vareps", [P, NT])
        rstd = sb("rstd", [P, NT])
        ln = sb("ln", [P, NT, E])
        tT_hi = sb("tT_hi", [P, TOK], F32R)
        tT_lo = sb("tT_lo", [P, TOK], F32R)
        q_hi = sb("q_hi", [P, TOK], F32R)
        q_lo = sb("q_lo", [P, TOK], F32R)
        k_hi = sb("k_hi", [P, TOK], F32R)
        k_lo = sb("k_lo", [P, TOK], F32R)
        qs = sb("qs", [P, NG, TOK], F32R)
        ks = sb("ks", [P, NG, TOK], F32R)
        v_t = sb("v_t", [P, NT, H, VW])
        negmax = sb("negmax", [P, NT, H])
        nm_hi, nm_lo = q_hi[0:H, :], q_lo[0:H, :]
        prob = sb("prob", [P, 2, NJ, 3 * P])
        aT = prob[:, 0, :, :].rearrange("p j s -> p (j s)")[:, 0:TOK]
        attT = sb("attT", [P, 2, NG, S])
        rden = sb("rden", [P, NT, H])
        att = sb("att", [P, NT, E])
        x1 = sb("x1", [P, NT, E])
        x1b = att
        cmax = sb("cmax", [P, NT])
        csum = sb("csum", [P, NT])
        crec = sb("crec", [P, NT])
        cp = sb("cp", [P, NT, P])
        cpT_hi, cpT_lo = tT_hi, tT_lo
        sums = sb("sums", [P, 2, NT, E])
        x2, acc = sums[:, 0], sums[:, 1]
        w_in = sums[:, :, :, :].rearrange("p a k e -> p (a k) e")
        fT_hi = sb("fT_hi", [P, TOK], F32R)
        fT_lo = sb("fT_lo", [P, TOK], F32R)
        xT_hi, xT_lo = ({n: w[:, k * P:(k + 1) * P] for k, n in enumerate(("xwk", "xwv", "xwo"))}
                        for w in (fT_hi, fT_lo))
        hr = sb("hr", [P, 2, TOK])
        h_hi = sb("h_hi", [P, 3, TOK], F32R)
        h_lo = sb("h_lo", [P, 3, TOK], F32R)
        y_sb = sb("y_sb", [P, NE, TOK])
        stage = y_sb
        c_in = hr[:, :, :].rearrange("p b t -> p (b t)").rearrange("p (n e) -> p n e", e=E)
        (cT_hi, kp_hi, vp_hi), (cT_lo, kp_lo, vp_lo) = ([w[:, k, :] for k in range(3)] for w in (h_hi, h_lo))
        kc_lo = cT_lo[0:1, :]
        lgt = sb("lgt", [P, NT, NE])
        lmax = sb("lmax", [P, NT])
        above = sb("above", [P, NT, NE])
        xs = sb("xs", [P, NT, NE])
        lshift = sb("lshift", [P, NT])
        part = sb("part", [P, NT, NE])
        part2 = sb("part2", [P, NT, NE])
        part4 = sb("part4", [P, NT, 4])
        part8 = sb("part8", [P, NT, 2])
        crec2 = sb("crec2", [P, NT])
        mass = sb("mass", [P, NT])
        shift = sb("shift", [P, NT])
        gate0 = sb("gate0", [P, NT, NE])
        gate = sb("gate", [P, NT, NE])

        sbuf_s = ps("sbuf_s", [P, NJ, TOK])
        sbuf_m = ps("sbuf_m", [P, TOK])
        h_ps = ps("h_ps", [P, 2, TOK])
        y_ps = ps("y_ps", [P, TOK])
        ps_of = {"s": sbuf_s[:, 0, :], "t": sbuf_s[:, 2, :], "m": sbuf_m[:, :],
                 "u": h_ps[:, 0, :], "v": h_ps[:, 1, :], "y": y_ps[:, :]}
        halves = {"s": sbuf_s[:, 0:2, :], "t": sbuf_s[:, 2:4, :]}

        x_loaded = sem("x_loaded")
        xr_loaded = sem("xr_loaded")
        wq_loaded = sem("wq_loaded")
        w_loaded = sem("w_loaded")
        c_loaded = sem("c_loaded")
        w1_loaded = sem("w1_loaded")
        w2_loaded = sem("w2_loaded")
        ident_made = sem("ident_made")
        mask_base = sem("mask_base")
        const_made = sem("const_made")
        set_full = sem("set_full")
        set_hi = sem("set_hi")
        set_free = sem("set_free")
        table_hi = sem("table_hi")
        w1_hi_made = sem("w1_hi_made")
        w1_lo_made = sem("w1_lo_made")
        w2_hi_made = sem("w2_hi_made")
        w2_lo_made = sem("w2_lo_made")
        small_hi = sem("small_hi")
        small_lo = sem("small_lo")
        kc_placed = sem("kc_placed")
        dve_step = sem("dve_step")
        pool_step = sem("pool_step")
        full = {b: sem(f"full_{b}") for b in BUFFERS}
        free = {b: sem(f"free_{b}") for b in BUFFERS}
        var_made = {k: sem(f"var_made_{k}") for k in "za"}
        vareps_made = {k: sem(f"vareps_made_{k}") for k in "za"}
        rstd_made = {k: sem(f"rstd_made_{k}") for k in "za"}
        normed = {k: sem(f"normed_{k}") for k in "za"}
        hi_made = {k: sem(f"hi_made_{k}") for k in "za"}
        ta_lo_made = sem("ta_lo_made")
        stacked = sem("stacked")
        nm_stacked = [sem(f"nm_stacked_{b}") for b in range(2)]
        nm_cleared = sem("nm_cleared")
        mask_turn = sem("mask_turn")
        prob_made = sem("prob_made")
        cmax_made = sem("cmax_made")
        x1b_made = sem("x1b_made")
        h_full = sem("h_full")
        h_free = sem("h_free")
        hr_made = sem("hr_made")
        hlo_made = sem("hlo_made")
        second_done = sem("second_done")
        y_free = sem("y_free")
        above_made = sem("above_made")
        acc_begun = sem("acc_begun")
        gate_turn = sem("gate_turn")
        gate_made = sem("gate_made")
        stored = sem("stored")

        block = ctx.enter_context(nc.Block())

        def filled(eng, ph, step):
            eng.wait_ge(full[step[3]], ph.fill(step) + 1)

        def drained(eng, ph, name, n=0):
            step = ph.find(name, n)
            eng.wait_ge(free[step[3]], ph.fill(step) + 1)

        def words(ap):
            return ap.bitcast(F32)

        def pair_of_heads(n):
            return prob[:, n // 2 % 2, 2 * (n % 2):2 * (n % 2) + 2, :]

        def blocks(ap, first):
            b = ap.rearrange("p (c t) -> p c t", t=P)
            return b[:, 0:3:2, :] if first else b[:, 1, :]

        def as_w2(ap):
            return ap.rearrange("p n f -> p (n f)").rearrange("p (c d) -> p c d", d=E)

        SPLIT = {"T1": ("z", 0, 3), "Q": ("z", 1, 3), "K": ("z", 2, 3),
                 "TA": ("a", 0, 4), "T2": ("a", 1, 4), "PT": ("a", 2, 4), "T3": ("a", 3, 4)}
        SPLIT_BUF = {"T1": (tT_hi, tT_lo), "Q": (q_hi, q_lo), "K": (k_hi, k_lo), "TA": (tT_hi, tT_lo),
                     "T2": (tT_hi, tT_lo), "PT": (cpT_hi, cpT_lo), "T3": (fT_hi, fT_lo)}
        SPLIT_SCALE = {"K": K_SCALE}
        STACK_DMAS = 2 * 3 * NG
        SQUARE = {"wo": 3, "xwk": 4, "xwv": 5, "xwo": 6}

        def hi_wait(eng, ph, name):
            k, at, n = SPLIT[name]
            pair = ph.z if k == "z" else ph.a
            eng.wait_ge(hi_made[k], pair * n + at + 1)

        @block.sync
        def _(sp):
            def row(v):
                return v.rearrange("(a e) -> a e", a=1)

            sp.dma_start(x_t[:, :, :], x_v[:, 0:NT, :]).then_inc(x_loaded, 16)
            for n, w in enumerate([wq, wk, wv]):
                sp.dma_start(w_in[:, n, :], w).then_inc(wq_loaded, 16)
            for n, v in enumerate([gamma, beta, xbv, xbq]):
                sp.dma_start(vec_rows[n:n + 1, :], row(v)).then_inc(wq_loaded, 16)
            for n, w in enumerate([wo, xwk, xwv, xwo, xwq]):
                sp.dma_start(w_in[:, 3 + n, :], w).then_inc(w_loaded, 16)
            sp.dma_start(bias_rows[0:CHUNKS, :], b1.rearrange("n (c p) -> (n c) p", p=P)).then_inc(w_loaded, 16)
            sp.dma_start(bias_rows[CHUNKS:CHUNKS + NE, :], b2).then_inc(w_loaded, 16)
            sp.dma_start(wr_in[:, :], wr).then_inc(w_loaded, 16)
            sp.dma_start(xbo_b[:, :], row(xbo).to_broadcast([P, E])).then_inc(w_loaded, 16)
            sp.dma_start(br_b[:, :], row(br).to_broadcast([P, NE])).then_inc(w_loaded, 16)
            sp.dma_start(c_in[:, :, :], ctx_v).then_inc(c_loaded, 16)
            sp.dma_start(stage[:, :, :], w1.rearrange("n d f -> d n f")).then_inc(w1_loaded, 16)
            sp.wait_ge(const_made, 8)

            def stack_rows(ph, name):
                hi, lo = SPLIT_BUF[name]
                to, order = (qs, (hi, lo, hi)) if name == "Q" else (ks, (hi, hi, lo))
                drained(sp, ph, name)
                for r, src in enumerate(order):
                    for g in range(NG):
                        sp.dma_start(words(to[r:P:4, g, :]), words(src[g * 32:(g + 1) * 32, :])).then_inc(stacked, 16)

            def nm_rows(ph, b):
                drained(sp, ph, "MT", b)
                t = slice(b * S, (b + 1) * S)
                for g in range(NG):
                    for r, src in enumerate((nm_hi, nm_lo)):
                        sp.dma_start(words(qs[3 + 4 * r:P:ROWS, g, t]), words(src[g * NJ:(g + 1) * NJ, t]))\
                          .then_inc(nm_stacked[b], 16)

            def step(ph, s):
                name, n = s[1:3]
                if name == "V":
                    stack_rows(ph, "Q")
                    stack_rows(ph, "K")
                if name == "MT":
                    nm_rows(ph, n)
                if (name, n) == ("SC", 15):
                    filled(sp, ph, s)
                    for r in range(2):
                        sp.dma_start(words(qs[3 + 4 * r:P:ROWS, :, :]), zeros[:, :, :].to_broadcast([NJ, NG, TOK]))\
                          .then_inc(nm_cleared, 16)
                if (name, n) == ("GA", NE // 2 - 1):
                    drained(sp, ph, name, n)
                    sp.dma_start(out_v[:, bass.ts(ph.f, NT), :], acc).then_inc(stored, 16)
                if name == "kc":
                    drained(sp, ph, name, n)
                    sp.dma_start(words(kc[1:2, n * TOK:(n + 1) * TOK]), words(kc_lo)).then_inc(kc_placed, 16)
                if (name, n) == ("vo", 1):
                    sp.wait_ge(w1_hi_made, 1)
                    sp.wait_ge(w1_lo_made, 1)
                    sp.dma_start(as_w2(stage[:, :, :]), w2.rearrange("n (c p) d -> p (n c) d", p=P)).then_inc(w2_loaded, 16)

            def body(ph):
                if "Z" in ph.parts and ph.a is not None:
                    sp.wait_ge(normed["z"], ph.z)
                    sp.dma_start(x_t[:, :, :], x_v[:, bass.ts(ph.z, NT), :]).then_inc(x_loaded, 16)
                if "A" in ph.parts:
                    if ph.f is not None:
                        sp.wait_ge(free["m"], ph.before["m"])
                    sp.dma_start(x_r[:, :, :], x_v[:, bass.ts(ph.a, NT), :]).then_inc(xr_loaded, 16)
                for t in range(SLOTS):
                    for s in ph.steps(t):
                        step(ph, s)

            run_phases(sp, body)
            sp.wait_ge(nm_cleared, 32 * NP)
            sp.wait_ge(stored, 16 * NP + 16)

        @block.gpsimd
        def _(pool):
            pool.memset(ident[:, :], 0.0).then_inc(ident_made, 1)
            pool.wait_ge(ident_made, 1)
            pool.affine_select(out=ident[:, :], in_=ident[:, :], compare_op=ALU.not_equal, fill=1.0, base=0,
                               pattern=[[-1, P]], channel_multiplier=1).then_inc(ident_made, 1)
            pool.memset(eps_t[:, :], LN_EPS).then_inc(mask_base, 1)
            pool.memset(minus_half[:, :], -0.5).then_inc(mask_base, 1)
            pool.wait_ge(mask_base, 2)
            steps_done = [0]

            def mark(ins):
                steps_done[0] += 1
                ins.then_inc(pool_step, 1)

            def settle():
                pool.wait_ge(pool_step, steps_done[0])

            def masks():
                pool.memset(words(qs[:, :, :]), 0.0).then_inc(const_made, 1)
                pool.memset(words(ks[:, :, :]), 1.0).then_inc(const_made, 1)
                pool.memset(v_t[:, :, :, :], 0.0).then_inc(mask_base, 1)
                pool.memset(causal[:, :, :], 0.0).then_inc(mask_base, 1)
                pool.wait_ge(mask_base, 4)
                pool.memset(v_t[:, :, :, D:D + 1], 1.0).then_inc(const_made, 1)
                pool.tensor_copy(ident_bf[:, :], ident[:, :]).then_inc(const_made, 1)
                pool.affine_select(out=causal[:, :, :], in_=causal[:, :, :], compare_op=ALU.is_ge, fill=MASKED,
                                   base=0, pattern=[[0, NG], [-1, P]], channel_multiplier=1).then_inc(const_made, 1)
                pool.memset(cp[:, :, :], 0.0).then_inc(const_made, 1)
                pool.memset(zeros[:, :, :], 0.0).then_inc(const_made, 1)
                pool.memset(words(ones_r[:, :]), 1.0).then_inc(const_made, 1)

            def mask(ph, s):
                drained(pool, ph, "SC", s[2])
                pool.sem_inc(mask_turn, 1)
                v = pair_of_heads(s[2])[:, :, 0:2 * P]
                pool.affine_select(out=v, in_=v, compare_op=ALU.is_ge, fill=0.0, base=0,
                                   pattern=[[0, 2], [0, 2], [1, P]], channel_multiplier=-1).then_inc(prob_made, 1)

            def inverse_deviation(k, at):
                pool.wait_ge(var_made[k], at * NT + NT)
                pool.tensor_tensor(vareps[:, :], mv[:, :, 1], eps_t[:, :], ALU.add).then_inc(vareps_made[k], 1)
                pool.wait_ge(vareps_made[k], at + 1)
                pool.tensor_tensor(rstd[:, :], vareps[:, :], minus_half[:, :], ALU.pow).then_inc(rstd_made[k], 1)

            def bisect(it):
                width = WIDTH * 0.5 ** (it + 1)
                settle()
                mark(pool.tensor_scalar(part[:, :, :], above[:, :, :], width, 0.0, ALU.subtract, ALU.max))
                settle()
                mark(pool.tensor_tensor(part2[:, :, :], part[:, :, :], part[:, :, :], ALU.mult))
                settle()
                mark(pool.tensor_tensor(part4[:, :, :], part2[:, :, 0:4], part2[:, :, 4:8], ALU.add))
                settle()
                mark(pool.tensor_tensor(part8[:, :, :], part4[:, :, 0:2], part4[:, :, 2:4], ALU.add))
                settle()
                mark(pool.tensor_tensor(mass[:, :], part8[:, :, 0], part8[:, :, 1], ALU.add))
                settle()
                if it < BISECTIONS - 1:
                    mark(pool.tensor_scalar(shift[:, :], mass[:, :], 1.0, width, ALU.is_ge, ALU.mult))
                    settle()
                    mark(pool.tensor_tensor(above[:, :, :], above[:, :, :],
                                            shift[:, :].unsqueeze(2).to_broadcast([P, NT, NE]), ALU.subtract))
                else:
                    pool.sem_inc(gate_turn, 1)

            def step(ph, s):
                name, n = s[1:3]
                if name == "SC":
                    mask(ph, s)
                if name == "T1":
                    pass
                if (name, n) == ("BT", 3):
                    inverse_deviation("a", ph.a * 3)
                if name == "WO":
                    inverse_deviation("a", ph.a * 3 + 1)
                    drained(pool, ph, "WO")
                    pool.tensor_tensor(x1b[:, :, :], x1[:, :, :], xbo_b[:, :].unsqueeze(1).to_broadcast([P, NT, E]),
                                       ALU.add).then_inc(x1b_made, 1)
                if name == "XO":
                    inverse_deviation("a", ph.a * 3 + 2)

            def body(ph):
                if ph.a is None and ph.f is None:
                    inverse_deviation("z", ph.z)
                    masks()
                    return
                for t in range(SLOTS):
                    if "Z" in ph.parts and t == LN_Z:
                        inverse_deviation("z", ph.z)
                    if "X" in ph.parts:
                        if t == 1:
                            pool.wait_ge(above_made, ph.f + 1)
                            pool.sem_inc(mask_turn, 1)
                        if t == 2:
                            pool.wait_ge(stored, ph.f * 16 + 16)
                            pool.sem_inc(mask_turn, 1)
                            pool.tensor_copy(acc, x2).then_inc(acc_begun, 1)
                        if BISECT_FROM <= t < BISECT_FROM + BISECTIONS:
                            bisect(t - BISECT_FROM)
                    for s in ph.steps(t):
                        step(ph, s)
                settle()
                pool.sem_clear(pool_step)
                steps_done[0] = 0

            run_phases(pool, body)

        @block.tensor
        def _(pe):
            def three(out_ap, w_hi, w_lo, m_hi, m_lo, start=True, stop=True):
                pe.matmul(out_ap, w_hi, m_lo, start=start, stop=False)
                pe.matmul(out_ap, w_lo, m_hi, start=False, stop=False)
                return pe.matmul(out_ap, w_hi, m_hi, start=False, stop=stop)

            pe.wait_ge(ident_made, 2)
            pe.wait_ge(wq_loaded, 16 * 7)
            for n in range(3):
                pe.transpose(sbuf_s[:, n, 0:P], w_in[:, n, :], ident[:, :])
            pe.transpose(sbuf_s[:, 3, 0:4], vec_rows[:, :], ident[0:4, 0:4]).then_inc(set_full, 1)
            pe.wait_ge(set_free, 1)

            def transposes(dst, src):
                for k in range(NT):
                    last = pe.transpose(dst[:, k * P:(k + 1) * P], src[:, k, :], ident[:, :])
                return last

            def project_rows(dst, t_hi, t_lo, w_hi, w_lo):
                for k in range(NT):
                    w = slice(k * P, (k + 1) * P)
                    last = three(dst[:, w], t_hi[:, w], t_lo[:, w], w_hi, w_lo)
                return last

            def max_scores(ph, n, dst):
                b, kind = divmod(n // 2, 3)
                tile = 2 * b + (kind > 0)
                if n == 0:
                    pe.wait_ge(stacked, (ph.z + 1) * 16 * STACK_DMAS)
                    if ph.a is not None:
                        pe.wait_ge(nm_cleared, ph.z * 32)
                    else:
                        pe.wait_ge(const_made, 8)
                gs, width = (range(NG), P) if kind == 0 else (range(2 * kind - 2, 2 * kind), S)
                for at, g in enumerate(gs):
                    for j in range(2):
                        r = slice(ROWS * (2 * (n % 2) + j), ROWS * (2 * (n % 2) + j + 1))
                        pe.matmul(dst[:, j, at * width:(at + 1) * width],
                                  qs[r, g, tile * P:(tile + 1) * P], ks[r, g, b * S:b * S + width],
                                  start=(at == 0), stop=True, skip_group_check=(at > 0))
                for j in range(2):
                    diagonal = dst[:, j, :].rearrange("p (g s) -> p g s", s=width)[:, :, width - P:width]
                    last = pe.matmul(diagonal, ident_bf[:, :], causal[:, 0:len(gs), :],
                                     start=False, stop=True, skip_group_check=True)
                return last

            def scores(ph, n, dst):
                b, g = divmod(n // 2, NG)
                if n % 8 == 0:
                    pe.wait_ge(nm_stacked[b], ph.a * 128 + 128)
                for first in (True, False):
                    for j in range(2):
                        r = slice(ROWS * (2 * (n % 2) + j), ROWS * (2 * (n % 2) + j + 1))
                        k0, q0, w = (0, 0, S) if first else (P, P, P)
                        last = pe.matmul(blocks(dst[:, j, 0:3 * P], first), ks[r, g, b * S + k0:b * S + k0 + P],
                                         qs[r, g, b * S + q0:b * S + q0 + w], start=True, stop=True)
                return last

            def values(ph, n, dst):
                b, g = divmod(n, NG)
                pe.wait_ge(prob_made, ph.a * 16 + 2 * n + 2)
                for first in (True, False):
                    for j in range(NJ):
                        o = dst[VW * j:VW * (j + 1), :]
                        last = pe.matmul(o[:, 0:S] if first else o[:, P:S], v_t[:, 2 * b + (not first), g * NJ + j, :],
                                         blocks(prob[:, n % 2, j, :], first), start=first, stop=True,
                                         skip_group_check=not first)
                return last

            def step(ph, s):
                t, name, n, buf = s
                before = ph.fill(s)
                if not (isinstance(before, int) and before == 0):
                    pe.wait_ge(free[buf], before)
                dst = ps_of[buf]
                if name == "T1":
                    pe.wait_ge(normed["z"], ph.z + 1)
                    last = transposes(dst, ln)
                if name in ("TA", "T2", "T3"):
                    pe.wait_ge(normed["a"], ph.a * 3 + ("TA", "T2", "T3").index(name) + 1)
                    last = transposes(dst, ln)
                if name in ("Q", "K"):
                    drained(pe, ph, "T1")
                    w = "QK".index(name)
                    last = three(dst, wT_hi[:, w, :], wT_lo[:, w, :], tT_hi[:, :], tT_lo[:, :])
                if name == "V":
                    last = project_rows(dst, tT_hi, tT_lo, wT_hi[:, 2, :], wT_lo[:, 2, :])
                if name == "MAX":
                    last = max_scores(ph, n, halves[buf])
                if name == "MT":
                    drained(pe, ph, "MAX", 6 * n + 4)
                    drained(pe, ph, "MAX", 6 * n + 5)
                    for k in range(2 * n, 2 * n + 2):
                        last = pe.transpose(dst[0:H, k * P:(k + 1) * P], negmax[:, k, :], ident[:, :])
                if name == "SC":
                    last = scores(ph, n, halves[buf])
                if name == "PV":
                    last = values(ph, n, dst)
                if name == "BT":
                    b, k = divmod(n, 2)
                    if ph.find("PV", 0)[3] != ph.find("PV", 1)[3]:
                        drained(pe, ph, "PV", 4 * b + 2)
                    drained(pe, ph, "PV", 4 * b + 3)
                    for g in range(NG):
                        last = pe.transpose(dst[:, g * P:(g + 1) * P], attT[:, b, g, k * P:(k + 1) * P], ident[:, :])
                if name == "WO":
                    pe.wait_ge(ta_lo_made, ph.a + 1)
                    last = project_rows(dst, tT_hi, tT_lo, wT_hi[:, 3, :], wT_lo[:, 3, :])
                if name == "XS":
                    drained(pe, ph, "T2")
                    if ph.once:
                        pe.wait_ge(kc_placed, 32)
                    for k in range(NT):
                        w = slice(k * P, (k + 1) * P)
                        c = bass.ds(ph.a * P + (k // 2) * C, C)
                        o = dst[:, k * C:(k + 1) * C]
                        three(o, tT_hi[:, w], tT_lo[:, w], ka_hi[:, c], ka_lo[:, c], stop=False)
                        last = pe.matmul(o, ones_r[:, :], kc[:, c], start=False, stop=True)
                if name == "PT":
                    drained(pe, ph, "XS")
                    last = transposes(dst, cp)
                if name == "XO":
                    drained(pe, ph, "PT")
                    for k in range(NT):
                        w = slice(k * P, (k + 1) * P)
                        v = bass.ds(ph.a, 1)
                        last = three(dst[:, w], cpT_hi[:, w], cpT_lo[:, w], vo_hi[:, v, :], vo_lo[:, v, :])
                if name == "LG":
                    for k in range(NT):
                        w = slice(k * P, (k + 1) * P)
                        last = three(dst[:, k * NE:(k + 1) * NE], fT_hi[:, w], fT_lo[:, w], wr_hi[:, :], wr_lo[:, :])
                if name == "GA":
                    pe.wait_ge(y_free, ph.f * NE + 2 * n + 2)
                    for e in range(2):
                        for k in range(NT):
                            w = slice(k * P, (k + 1) * P)
                            last = pe.transpose(halves[buf][:, e, w], y_sb[:, 2 * n + e, w], ident[:, :])
                if (name, n) == ("wo", 0):
                    pe.wait_ge(w_loaded, 16 * 10)
                if name in SQUARE:
                    last = pe.transpose(dst[:, 0:P], w_in[:, SQUARE[name], :], ident[:, :])
                if name == "bias":
                    last = pe.transpose(dst[:, 0:CHUNKS + NE], bias_rows[:, :], ident[0:CHUNKS + NE, 0:CHUNKS + NE])
                if name == "cT":
                    pe.wait_ge(c_loaded, 16)
                    last = transposes(dst, c_in[:, n * NT:(n + 1) * NT, :])
                if name in ("kp", "vp"):
                    w = "xw" + name[0]
                    drained(pe, ph, "cT", n)
                    last = three(dst, xT_hi[w], xT_lo[w], cT_hi, cT_lo)
                if name == "ka":
                    drained(pe, ph, "vp", n)
                    pe.wait_ge(small_lo, 2)
                    last = three(dst, xwq_hi[:, :], xwq_lo[:, :], kp_hi, kp_lo)
                if name == "kc":
                    last = three(dst[0:2, :], bq_hi[:, :], bq_lo[:, :], kp_hi, kp_lo)
                if name == "vo":
                    last = project_rows(dst, vp_hi, vp_lo, xT_hi["xwo"], xT_lo["xwo"])
                last.then_inc(full[buf], 1)

            def first_product(ph, c):
                e, fb = divmod(c, FB)
                if c == 0:
                    pe.wait_ge(free["m"], ph.before["m"])
                    for b in "uvy":
                        pe.wait_ge(free[b], ph.before[b])
                    pe.wait_ge(w1_lo_made, 1)
                    pe.wait_ge(w2_lo_made, 1)
                if 2 <= c < DVE_BLOCKS + 2:
                    pe.wait_ge(hr_made, ph.f * DVE_BLOCKS + c - 1)
                if c >= DVE_BLOCKS + 2:
                    pe.wait_ge(h_free, ph.f * CHUNKS + c - 1)
                w = slice(fb * P, (fb + 1) * P)
                three(h_ps[:, c % 2, :], w1_hi[:, e, w], w1_lo[:, e, w], fT_hi[:, :], fT_lo[:, :]).then_inc(h_full, 1)

            def second_product(ph, c):
                e, fb = divmod(c, FB)
                pe.wait_ge(hlo_made, ph.f * CHUNKS + c + 1)
                if fb == 0 and e > 0:
                    pe.wait_ge(y_free, ph.f * NE + e)
                three(y_ps[:, :], w2_hi[:, c, :], w2_lo[:, c, :], h_hi[:, c % 3, :], h_lo[:, c % 3, :],
                      start=(fb == 0), stop=(fb == FB - 1)).then_inc(second_done, 1)

            def body(ph):
                for t in range(SLOTS):
                    if "X" in ph.parts and t < CHUNKS:
                        first_product(ph, t)
                    if "X" in ph.parts and 0 <= t - LAG < CHUNKS:
                        second_product(ph, t - LAG)
                    for s in ph.steps(t):
                        step(ph, s)

            run_phases(pe, body)

        @block.scalar
        def _(act):
            act.wait_ge(set_full, 1)
            act.activation(wT_hi[:, 0:2, :], sbuf_s[:, 0:2, 0:P], ACT.Copy)
            act.activation(wT_hi[:, 2, :].rearrange("p (h d) -> p h d", d=D),
                           sbuf_s[:, 2, 0:P].rearrange("p (d h) -> p h d", h=H), ACT.Copy)
            act.activation(vec[:, :], sbuf_s[:, 3, 0:4], ACT.Copy).then_inc(set_hi, 1)

            def table(ph, s):
                t, name, n, buf = s
                filled(act, ph, s)
                src = ps_of[buf]
                half = slice(n * TOK, (n + 1) * TOK)
                if name == "wo":
                    ins = act.activation(wT_hi[:, 3, :], src[:, 0:P], ACT.Copy)
                if name in xT_hi:
                    ins = act.activation(xT_hi[name], src[:, 0:P], ACT.Copy)
                if name == "bias":
                    act.activation(biasT[:, :], src[:, 0:CHUNKS + NE], ACT.Copy).then_inc(free[buf], 1)
                    return
                if name in ("cT", "kp"):
                    if (name, n) == ("cT", 1):
                        act.wait_ge(kc_placed, 16)
                    ins = act.activation(cT_hi if name == "cT" else kp_hi, src, ACT.Copy)
                if name == "vp":
                    ins = act.activation(vp_hi, src, ACT.Identity, bias=vec[:, 2:3])
                if name == "ka":
                    ins = act.activation(ka_hi[:, half], src, ACT.Copy, scale=C_SCALE)
                if name == "kc":
                    ins = act.activation(kc[0:1, half], src[0:1, :], ACT.Copy, scale=C_SCALE)
                if name == "vo":
                    ins = act.activation(vo_hi[:, n * NT:(n + 1) * NT, :], src.rearrange("p (n e) -> p n e", e=E), ACT.Copy)
                ins.then_inc(table_hi, 1)

            def step(ph, s):
                t, name, n, buf = s
                if (name, n) in W_ORDER:
                    table(ph, s)
                if name in SPLIT and name != "TA":
                    filled(act, ph, s)
                    if name == "Q" and ph.a is not None:
                        act.wait_ge(stacked, ph.z * 16 * STACK_DMAS)
                    act.activation(SPLIT_BUF[name][0][:, :], ps_of[buf], ACT.Copy,
                                   scale=SPLIT_SCALE.get(name, 1.0)).then_inc(hi_made[SPLIT[name][0]], 1)
                if name == "TA":
                    drained(act, ph, "TA")
                    act.activation(tT_hi[:, :], aT, ACT.Copy).then_inc(hi_made["a"], 1)
                if name == "SC":
                    filled(act, ph, s)
                    if n >= 4:
                        filled(act, ph, ph.find("PV", n // 2 - 2))
                    act.activation(pair_of_heads(n), halves[buf][:, :, 0:3 * P], ACT.Exp).then_inc(free[buf], 1)
                if name == "PV":
                    filled(act, ph, s)
                    act.activation(attT[:, n // NG, n % NG, :], ps_of[buf][:, 0:S], ACT.Copy).then_inc(free[buf], 1)
                if name == "XS":
                    act.wait_ge(cmax_made, ph.a + 1)
                    for k in range(NT):
                        h0 = (k // 2) * C
                        last = act.activation(cp[:, k, h0:h0 + C], ps_of[buf][:, k * C:(k + 1) * C], ACT.Exp,
                                              bias=cmax[:, k:k + 1], accum_out=csum[:, k:k + 1])
                    last.then_inc(free[buf], 1)

            def hidden(ph, c):
                bias = biasT[:, c:c + 1]
                if c >= DVE_BLOCKS:
                    act.wait_ge(h_full, ph.f * CHUNKS + c + 1)
                    act.wait_ge(hlo_made, ph.f * CHUNKS + c - 1)
                    act.activation(hr[:, c % 2, :], h_ps[:, c % 2, :], ACT.Relu, bias=bias)
                if c >= 3:
                    act.wait_ge(second_done, ph.f * CHUNKS + c - 2)
                if c >= DVE_BLOCKS:
                    act.activation(h_hi[:, c % 3, :], h_ps[:, c % 2, :], ACT.Relu, bias=bias).then_inc(h_free, 1)
                else:
                    act.wait_ge(hr_made, ph.f * DVE_BLOCKS + c + 1)
                    act.activation(h_hi[:, c % 3, :], hr[:, c % 2, :], ACT.Copy).then_inc(h_free, 1)

            def evacuate_y(ph, e):
                act.wait_ge(second_done, ph.f * CHUNKS + FB * (e + 1))
                act.activation(y_sb[:, e, :], y_ps[:, :], ACT.Identity,
                               bias=biasT[:, CHUNKS + e:CHUNKS + e + 1]).then_inc(y_free, 1)

            def body(ph):
                for t in range(SLOTS):
                    if "X" in ph.parts and t < CHUNKS:
                        hidden(ph, t)
                    c = t - LAG
                    if "X" in ph.parts and 0 <= c < CHUNKS and c % FB == FB - 1:
                        evacuate_y(ph, c // FB)
                    for s in ph.steps(t):
                        step(ph, s)
                    if "W" in ph.parts and t == 8:
                        act.wait_ge(w_loaded, 16 * 10)
                        act.activation(xwq_hi[:, :], w_in[:, 7, :], ACT.Copy)
                        act.activation(wr_hi[:, :], wr_in[:, :], ACT.Copy).then_inc(small_hi, 1)
                    if "W" in ph.parts and t == 15:
                        act.wait_ge(w1_loaded, 16)
                        act.activation(w1_hi[:, :, :], stage[:, :, :], ACT.Copy).then_inc(w1_hi_made, 1)
                    if ph.once and "A" in ph.parts and t == 12:
                        act.wait_ge(w2_loaded, 16)
                        act.activation(w2_hi[:, :, :], as_w2(stage[:, :, :]), ACT.Copy).then_inc(w2_hi_made, 1)

            run_phases(act, body)

        @block.vector
        def _(dve):
            steps_done = [0]

            def mark(ins):
                steps_done[0] += 1
                ins.then_inc(dve_step, 1)

            def settle():
                dve.wait_ge(dve_step, steps_done[0])

            dve.sem_inc(stored, 16)

            def setup():
                dve.wait_ge(set_hi, 1)
                dve.tensor_tensor(wT_lo[:, 0:2, :], sbuf_s[:, 0:2, 0:P], wT_hi[:, 0:2, :], ALU.subtract)
                dve.tensor_tensor(wT_lo[:, 2, :].rearrange("p (h d) -> p h d", d=D),
                                  sbuf_s[:, 2, 0:P].rearrange("p (d h) -> p h d", h=H),
                                  wT_hi[:, 2, :].rearrange("p (h d) -> p h d", d=D), ALU.subtract).then_inc(set_free, 1)
                mark(dve.tensor_copy(bq_hi[:, 0:1], vec[:, 3:4]))
                mark(dve.tensor_copy(bq_hi[:, 1:2], vec[:, 3:4]))
                settle()
                dve.tensor_tensor(bq_lo[:, 0:1], vec[:, 3:4], bq_hi[:, 0:1], ALU.subtract)
                dve.tensor_tensor(bq_lo[:, 1:2], vec[:, 3:4], bq_hi[:, 0:1], ALU.subtract).then_inc(small_lo, 0 + 1)

            def table(ph, s):
                t, name, n, buf = s
                if name == "bias":
                    return
                dve.wait_ge(table_hi, [w for w in W_ORDER if w[0] != "bias"].index((name, n)) + 1)
                src = ps_of[buf]
                half = slice(n * TOK, (n + 1) * TOK)
                if name == "wo":
                    ins = dve.tensor_tensor(wT_lo[:, 3, :], src[:, 0:P], wT_hi[:, 3, :], ALU.subtract)
                if name in xT_hi:
                    ins = dve.tensor_tensor(xT_lo[name], src[:, 0:P], xT_hi[name], ALU.subtract)
                if name == "cT":
                    ins = dve.tensor_tensor(cT_lo, src, cT_hi, ALU.subtract)
                if name == "kp":
                    ins = dve.tensor_tensor(kp_lo, src, kp_hi, ALU.subtract)
                if name == "vp":
                    ins = dve.scalar_tensor_tensor(out=vp_lo, in0=src, scalar=vec[:, 2:3], in1=vp_hi,
                                                   op0=ALU.add, op1=ALU.subtract)
                if name == "ka":
                    ins = dve.scalar_tensor_tensor(out=ka_lo[:, half], in0=src, scalar=C_SCALE,
                                                   in1=ka_hi[:, half], op0=ALU.mult, op1=ALU.subtract)
                if name == "kc":
                    ins = dve.scalar_tensor_tensor(out=kc_lo, in0=src[0:1, :], scalar=C_SCALE,
                                                   in1=kc[0:1, half], op0=ALU.mult, op1=ALU.subtract)
                if name == "vo":
                    ins = dve.tensor_tensor(vo_lo[:, n * NT:(n + 1) * NT, :], src.rearrange("p (n e) -> p n e", e=E),
                                            vo_hi[:, n * NT:(n + 1) * NT, :], ALU.subtract)
                ins.then_inc(free[buf], 1)

            def layer_norm(k, at, src):
                for n in range(NT):
                    mark(dve.bn_stats(st6[:, n, :], src[:, n, :]))
                settle()
                for n in range(NT):
                    dve.bn_aggr(mv[:, n, :], st6[:, n, :]).then_inc(var_made[k], 1)
                dve.wait_ge(rstd_made[k], at + 1)
                for n in range(NT):
                    ins = dve.tensor_scalar(ln[:, n, :], src[:, n, :], mv[:, n, 0:1], rstd[:, n:n + 1],
                                            ALU.subtract, ALU.mult)
                ins.then_inc(normed[k], 1)

            def step(ph, s):
                t, name, n, buf = s
                src = ps_of[buf]
                if (name, n) in W_ORDER:
                    table(ph, s)
                if name in SPLIT and name != "TA":
                    hi, lo = SPLIT_BUF[name]
                    hi_wait(dve, ph, name)
                    if name in SPLIT_SCALE:
                        ins = dve.scalar_tensor_tensor(out=lo[:, :], in0=src, scalar=SPLIT_SCALE[name], in1=hi[:, :],
                                                       op0=ALU.mult, op1=ALU.subtract)
                    else:
                        ins = dve.tensor_tensor(lo[:, :], src, hi[:, :], ALU.subtract)
                    ins.then_inc(free[buf], 1)
                if name == "V":
                    filled(dve, ph, s)
                    if ph.a is None:
                        dve.wait_ge(const_made, 8)
                    dve.tensor_copy(v_t[:, :, :, 0:D], src.rearrange("p (k h d) -> p k h d", h=H, d=D))\
                       .then_inc(free[buf], 1)
                if name == "MAX":
                    filled(dve, ph, s)
                    b, kind = divmod(n // 2, 3)
                    tile = 2 * b + (kind > 0)
                    heads = slice(0, H) if kind == 0 else slice(8 * (kind - 1), 8 * kind)
                    j = 2 * (n % 2)
                    dve.tensor_reduce(negmax[:, tile, heads].rearrange("p (g j) -> p j g", j=NJ)[:, j:j + 2, :],
                                      halves[buf].rearrange("p j (g s) -> p j g s", g=NG if kind == 0 else 2),
                                      AX.X, ALU.max, negate=True).then_inc(free[buf], 1)
                if name == "MT":
                    filled(dve, ph, s)
                    w = slice(n * S, (n + 1) * S)
                    mark(dve.tensor_copy(nm_hi[:, w], src[0:H, w]))
                    settle()
                    dve.tensor_tensor(nm_lo[:, w], src[0:H, w], nm_hi[:, w], ALU.subtract).then_inc(free[buf], 1)
                if name == "BT":
                    filled(dve, ph, s)
                    v = src.rearrange("p (h w) -> p h w", w=VW)
                    mark(dve.reciprocal(rden[:, n, :], v[:, :, D]))
                    settle()
                    dve.tensor_tensor(att[:, n, :].rearrange("p (h d) -> p h d", d=D), v[:, :, 0:D],
                                      rden[:, n, :].unsqueeze(2).to_broadcast([P, H, D]), ALU.mult).then_inc(free[buf], 1)
                    if n == 3:
                        drained(dve, ph, "BT", 3)
                        layer_norm("a", ph.a * 3, att)
                if name == "TA":
                    filled(dve, ph, s)
                    dve.tensor_scalar(aT, src, vec[:, 0:1], vec[:, 1:2], ALU.mult, ALU.add).then_inc(free[buf], 1)
                    hi_wait(dve, ph, "TA")
                    dve.tensor_tensor(tT_lo[:, :], aT, tT_hi[:, :], ALU.subtract).then_inc(ta_lo_made, 1)
                if name == "WO":
                    filled(dve, ph, s)
                    dve.wait_ge(xr_loaded, ph.a * 16 + 16)
                    dve.tensor_tensor(x1[:, :, :], x_r[:, :, :], src.rearrange("p (k e) -> p k e", e=E),
                                      ALU.add).then_inc(free[buf], 1)
                    drained(dve, ph, "WO")
                    layer_norm("a", ph.a * 3 + 1, x1)
                if name == "XS":
                    filled(dve, ph, s)
                    dve.tensor_reduce(cmax[:, :], src[:, 0:NT * C].rearrange("p (k c) -> p k c", c=C), AX.X,
                                      ALU.max, negate=True).then_inc(cmax_made, 1)
                if name == "XO":
                    drained(dve, ph, "XS")
                    mark(dve.reciprocal(crec[:, :], csum[:, :]))
                    settle()
                    filled(dve, ph, s)
                    dve.wait_ge(x1b_made, ph.a + 1)
                    if ph.f is not None:
                        dve.wait_ge(acc_begun, ph.f + 1)
                    for k in range(NT):
                        ins = dve.scalar_tensor_tensor(out=x2[:, k, :], in0=src[:, k * E:(k + 1) * E],
                                                       scalar=crec[:, k:k + 1], in1=x1b[:, k, :],
                                                       op0=ALU.mult, op1=ALU.add)
                    ins.then_inc(free[buf], 1)
                    drained(dve, ph, "XO")
                    layer_norm("a", ph.a * 3 + 2, x2)
                if name == "LG":
                    filled(dve, ph, s)
                    dve.tensor_tensor(lgt[:, :, :], src[:, 0:NT * NE].rearrange("p (k e) -> p k e", e=NE),
                                      br_b[:, :].unsqueeze(1).to_broadcast([P, NT, NE]), ALU.add).then_inc(free[buf], 1)
                    drained(dve, ph, "LG")
                    mark(dve.tensor_scalar(xs[:, :, :], lgt[:, :, :], 0.5, None, ALU.mult))
                    settle()
                    mark(dve.tensor_reduce(lmax[:, :], xs[:, :, :], AX.X, ALU.max))
                    settle()
                    mark(dve.tensor_scalar(lshift[:, :], lmax[:, :], -1.0, None, ALU.add))
                    settle()
                    dve.tensor_tensor(above[:, :, :], xs[:, :, :],
                                      lshift[:, :].unsqueeze(2).to_broadcast([P, NT, NE]), ALU.subtract)\
                       .then_inc(above_made, 1)
                if name == "GA":
                    if n == 0:
                        gates(ph)
                        dve.wait_ge(acc_begun, ph.f + 1)
                    else:
                        drained(dve, ph, "GA", n - 1)
                    filled(dve, ph, s)
                    for e in range(2):
                        for k in range(NT):
                            ins = dve.scalar_tensor_tensor(out=acc[:, k, :], in0=halves[buf][:, e, k * E:(k + 1) * E],
                                                           scalar=gate[:, k, 2 * n + e:2 * n + e + 1],
                                                           in1=acc[:, k, :], op0=ALU.mult, op1=ALU.add)
                        if e == 0:
                            mark(ins)
                            settle()
                    ins.then_inc(free[buf], 1)

            def gates(ph):
                dve.wait_ge(gate_turn, ph.f + 1)
                mark(dve.reciprocal(crec2[:, :], mass[:, :]))
                settle()
                mark(dve.tensor_tensor(gate0[:, :, :], part2[:, :, :],
                                       crec2[:, :].unsqueeze(2).to_broadcast([P, NT, NE]), ALU.mult))
                settle()
                mark(dve.scalar_tensor_tensor(out=gate[:, :, :], in0=gate0[:, :, :], scalar=1e-9,
                                              in1=gate0[:, :, :], op0=ALU.is_gt, op1=ALU.mult))
                settle()

            def hidden_relu(ph, c):
                if c >= 2:
                    dve.wait_ge(hlo_made, ph.f * CHUNKS + c - 1)
                dve.wait_ge(h_full, ph.f * CHUNKS + c + 1)
                dve.tensor_scalar(hr[:, c % 2, :], h_ps[:, c % 2, :], biasT[:, c:c + 1], 0.0, ALU.add, ALU.max)\
                   .then_inc(hr_made, 1)

            def hidden_lo(ph, c):
                dve.wait_ge(h_free, ph.f * CHUNKS + c + 1)
                dve.tensor_tensor(h_lo[:, c % 3, :], hr[:, c % 2, :], h_hi[:, c % 3, :], ALU.subtract)\
                   .then_inc(hlo_made, 1)

            def body(ph):
                for t in range(SLOTS):
                    if "X" in ph.parts and t < CHUNKS:
                        if t < DVE_BLOCKS:
                            hidden_relu(ph, t)
                        if 0 < t <= DVE_BLOCKS:
                            hidden_lo(ph, t - 1)
                        if t >= DVE_BLOCKS:
                            hidden_lo(ph, t)
                    if "Z" in ph.parts and t == LN_Z:
                        dve.wait_ge(x_loaded, ph.z * 16 + 16)
                        layer_norm("z", ph.z, x_t)
                        if ph.a is None:
                            setup()
                    for s in ph.steps(t):
                        step(ph, s)
                    if "W" in ph.parts and t == 8:
                        dve.wait_ge(small_hi, 1)
                        dve.tensor_tensor(wr_lo[:, :], wr_in[:, :], wr_hi[:, :], ALU.subtract)
                        dve.tensor_tensor(xwq_lo[:, :], w_in[:, 7, :], xwq_hi[:, :], ALU.subtract).then_inc(small_lo, 1)
                    if "W" in ph.parts and t == 15:
                        dve.wait_ge(w1_hi_made, 1)
                        dve.tensor_tensor(w1_lo[:, :, :], stage[:, :, :], w1_hi[:, :, :], ALU.subtract)\
                           .then_inc(w1_lo_made, 1)
                    if ph.once and "A" in ph.parts and t == 12:
                        dve.wait_ge(w2_hi_made, 1)
                        dve.tensor_tensor(w2_lo[:, :, :], as_w2(stage[:, :, :]), w2_hi[:, :, :], ALU.subtract)\
                           .then_inc(w2_lo_made, 1)
                settle()
                dve.sem_clear(dve_step)
                steps_done[0] = 0

            run_phases(dve, body)

_INS = ["x", "ctx_1024", "L0_attn_Wq", "L0_attn_Wk", "L0_attn_Wv", "L0_attn_Wo", "L0_attn_gamma", "L0_attn_beta",
        "L0_xattn_Wk", "L0_xattn_Wv", "L0_xattn_bv", "L0_xattn_Wq", "L0_xattn_bq", "L0_xattn_Wo", "L0_xattn_bo",
        "L0_ffn_Wr", "L0_ffn_br", "L0_ffn_W1", "L0_ffn_b1", "L0_ffn_W2", "L0_ffn_b2"]
_OUTS = [((B, S, E), "float32")]


def kernel(**inputs):
    import numpy as _np
    import concourse.bacc as _bacc
    from concourse import mybir as _mybir
    from concourse.bass_utils import run_bass_kernel_spmd as _run

    nc = _bacc.Bacc("TRN2", target_bir_lowering=False, num_devices=1)
    arrays, args = {}, []
    for name in _INS:
        a = _np.ascontiguousarray(inputs[name])
        arrays[f"in_{name}_dram"] = a
        args.append(nc.dram_tensor(f"in_{name}_dram", a.shape, _mybir.dt.from_np(a.dtype), kind="ExternalInput").ap())
    for i, (shape, dtype) in enumerate(_OUTS):
        dt = _mybir.dt.from_np(_np.dtype(dtype))
        args.append(nc.dram_tensor(f"out_{i}_dram", shape, dt, kind="ExternalOutput").ap())
    bass_decoder_layer(nc, *args)
    r = _run(nc, [arrays], core_ids=[0])
    return r.results[0]["out_0_dram"]
```

```python
import concourse.bass as bass
from concourse import mybir
from contextlib import ExitStack

F32 = mybir.dt.float32
F32R = mybir.dt.float32r
BF16 = mybir.dt.bfloat16
ALU = mybir.AluOpType
ACT = mybir.ActivationFunctionType
AX = mybir.AxisListType

P = 128
B, S, E = 16, 256, 128
C = 64
H, D = 16, 8
NE, F = 8, 512
FB = F // P
TOK = 2 * S
NT = TOK // P
NP = B * S // TOK
NG, NJ = 4, 4
ROWS = 4 * D
VW = 32
LN_EPS = 1e-5
K_SCALE = float(D) ** -0.5
C_SCALE = float(E) ** -0.5
MASKED = -1e30
BISECTIONS = 25
WIDTH = 1.0 - (1.0 / NE) ** 0.5
CHUNKS = NE * FB
DVE_BLOCKS = 11
RB = 3
HB = 3
EARLY = 4
LAG = 2
SLOTS = CHUNKS + LAG + 2

LN_Z = 1
Z_STEPS = [
    (2.5, "NZ", 0, "-"), (4, "T1", 0, "t"), (6, "Q", 0, "m"), (7.5, "K", 0, "m"), (11, "V", 0, "m"),
    (15, "MAX", 0, "s"), (17, "MAX", 1, "t"), (18, "MAX", 2, "s"), (19.5, "MAX", 3, "t"),
    (21.5, "MAX", 4, "s"), (21.5, "MAX", 5, "t"), (23, "MAX", 6, "s"), (23, "MT", 0, "m"),
    (24, "MAX", 7, "t"), (24.5, "MAX", 8, "s"), (25, "MAX", 9, "t"), (25.5, "MAX", 10, "s"),
    (28, "MAX", 11, "t"), (31.5, "MT", 1, "m"), (35, "SC", 0, "s"), (35.5, "SC", 1, "t"),
    (35.5, "SC", 2, "s"), (35.5, "SC", 3, "t"),
]
A_STEPS = [
    (2, "SC", 4, "s"), (2, "SC", 5, "t"), (2.5, "PV", 0, "m"), (3.5, "SC", 7, "t"),
    (3.5, "PV", 1, "m"), (4, "SC", 6, "s"), (5.5, "PV", 2, "m"), (5.5, "SC", 8, "s"),
    (5.5, "SC", 9, "t"), (5.5, "PV", 3, "m"), (6.5, "SC", 10, "s"), (6.5, "SC", 11, "t"),
    (6.5, "PV", 4, "m"), (6.5, "SC", 12, "s"), (7, "SC", 13, "t"), (7, "SC", 14, "s"),
    (7, "PV", 5, "m"), (7, "XR", 0, "-"), (7.5, "SC", 15, "t"), (7.5, "BT", 0, "s"),
    (8, "PV", 6, "s"), (8.5, "BT", 1, "m"), (9.5, "PV", 7, "m"), (10, "BT", 2, "m"),
    (12, "BT", 3, "m"), (13, "NA", 0, "-"), (15, "TA", 0, "m"), (17.5, "WO", 0, "m"),
    (18, "NA", 1, "-"), (21, "T2", 0, "m"), (25, "XS", 0, "m"), (26.5, "PT", 0, "m"),
    (28, "XO", 0, "m"), (28.5, "NA", 2, "-"), (33, "T3", 0, "m"),
]
X_STEPS = [
    (0.5, "LG", 0, "m"), (35.5, "GT", 0, "-"),
]
G_STEPS = [
    (1.5, "GA", 0, "s"), (10.5, "GA", 1, "t"), (11, "GA", 2, "s"), (13, "GA", 3, "t"),
]
SUM_AT = 24
BISECT_FROM = 2
FIRST_Z = [
    (0, "NZ", 0, "-"), (0.5, "T1", 0, "m"), (2, "Q", 0, "s"), (3, "K", 0, "t"), (3, "V", 0, "m"),
    (4, "wo", 0, "u"), (4, "xwk", 0, "v"), (4.2, "xwv", 0, "y"), (4.4, "xwo", 0, "m"),
    (5, "cT", 0, "s"), (5.2, "bias", 0, "t"), (5.5, "kp", 0, "u"), (5.7, "bo", 0, "v"),
    (7.5, "vp", 0, "y"), (7.7, "kc", 0, "u"), (8.5, "ka", 0, "m"), (9, "vo", 0, "s"),
    (9, "cT", 1, "t"), (10.5, "kp", 1, "u"), (11, "vp", 1, "y"), (12, "MAX", 0, "s"),
    (12, "MAX", 1, "t"), (12.1, "ka", 1, "m"), (13.5, "MAX", 2, "s"), (13.6, "kc", 1, "u"),
    (15, "MAX", 3, "t"), (16.1, "vo", 1, "v"), (16.5, "MAX", 4, "s"), (17, "MAX", 5, "t"),
    (19, "MAX", 6, "s"), (19, "MAX", 7, "t"), (20.5, "MT", 0, "m"), (20.5, "MAX", 8, "s"),
    (22, "MAX", 9, "t"), (22, "MAX", 10, "s"), (24.5, "MAX", 11, "t"), (26, "MT", 1, "m"),
    (26.5, "SC", 0, "s"), (27, "SC", 1, "t"), (27.5, "SC", 2, "s"), (27.5, "SC", 3, "t"),
]
FIRST_A = [
    (1, "NZ", 0, "-"), (1, "SC", 4, "s"), (1, "SC", 5, "t"), (1, "PV", 0, "m"), (1, "T1", 0, "v"),
    (1, "SC", 6, "s"), (2.5, "SC", 7, "t"), (2.5, "PV", 1, "u"), (3, "SC", 8, "s"),
    (3, "SC", 9, "t"), (3, "PV", 2, "m"), (3, "Q", 0, "y"), (5, "SC", 10, "s"), (6, "SC", 11, "t"),
    (6, "PV", 3, "u"), (7, "K", 0, "v"), (7, "PV", 4, "m"), (7.5, "SC", 12, "s"),
    (8, "SC", 13, "t"), (8.5, "SC", 14, "s"), (8.5, "SC", 15, "t"), (8.5, "PV", 5, "y"),
    (8.5, "BT", 0, "v"), (9.5, "PV", 6, "m"), (9.5, "BT", 1, "y"), (10.5, "XR", 0, "-"),
    (10.5, "PV", 7, "u"), (10.5, "V", 0, "u"), (12.5, "BT", 2, "v"), (12.5, "BT", 3, "y"),
    (15, "NA", 0, "-"), (17.5, "TA", 0, "m"), (20, "WO", 0, "m"), (20, "MAX", 0, "s"),
    (20.5, "NA", 1, "-"), (21.5, "MAX", 1, "t"), (22, "T2", 0, "m"), (22, "MAX", 2, "s"),
    (23, "MAX", 3, "t"), (23.5, "MAX", 4, "s"), (24, "XS", 0, "m"), (25, "MAX", 5, "t"),
    (25.5, "PT", 0, "m"), (26.5, "MAX", 6, "s"), (26.5, "MAX", 7, "t"), (27.5, "MT", 0, "u"),
    (28, "XO", 0, "m"), (28.5, "MAX", 8, "s"), (28.5, "MAX", 9, "t"), (29, "NA", 2, "-"),
    (30, "MAX", 10, "s"), (31, "MAX", 11, "t"), (31.5, "MT", 1, "v"), (32, "T3", 0, "m"),
    (33, "SC", 0, "s"), (33, "SC", 1, "t"), (33.5, "SC", 2, "s"), (33.5, "SC", 3, "t"),
]
W1_AT = (6, 7, 11, 11)
W2_AT = (10, 12, 12, 16)
FIRST_LN_Z = (0, 1)
TABLES = ("wo", "bo", "xwk", "xwv", "xwo", "bias", "cT", "kp", "vp", "ka", "kc", "vo")
W_ORDER = [s[1:3] for s in sorted(FIRST_Z, key=lambda s: s[0]) if s[1] in TABLES]


BUFFERS = "stmuvy"
NO_BUFFER = "-"


class Phase:

    KINDS = [("Z", "W"), ("A", "Z"), ("X", "A", "Z"), ("X", "A", "Z", "G"), ("X", "A", "G"), ("X", "G"), ("G",)]
    LOOP, ROUNDS = 3, NP - 3

    def __init__(self, kind, g=None, f=None, a=None, z=None):
        self.g, self.f, self.a, self.z = g, f, a, z
        self.parts = self.KINDS[kind]
        self.once = kind < 2
        self.ln_z = FIRST_LN_Z[kind] if kind < 2 else LN_Z
        self.before = {b: sum(self.count(k, b) * (self.ROUNDS if k == self.LOOP else 1) for k in range(kind))
                       for b in BUFFERS}
        if kind == self.LOOP:
            for b in BUFFERS:
                if self.count(kind, b):
                    self.before[b] = g * self.count(kind, b) + self.before[b]
        self.order = {b: [s[1:3] for s in self.all_steps(self.parts) if s[3] == b] for b in BUFFERS}

    @staticmethod
    def all_steps(parts):
        lists = {"X": X_STEPS, "A": A_STEPS, "Z": Z_STEPS, "G": G_STEPS}
        if "X" in parts or "G" in parts:
            steps = [s for p in "XAZG" if p in parts for s in lists[p]]
        else:
            steps = FIRST_A if "A" in parts else FIRST_Z
        return sorted(steps, key=lambda s: s[0])

    @classmethod
    def count(cls, kind, b):
        return sum(s[3] == b for s in cls.all_steps(cls.KINDS[kind]))

    def fill(self, step):
        return self.before[step[3]] + self.order[step[3]].index(step[1:3])

    def find(self, name, n=0):
        return next(s for s in self.all_steps(self.parts) if s[1:3] == (name, n))

    def steps(self, slot):
        return [s for s in self.all_steps(self.parts) if int(s[0]) == slot]


def run_phases(eng, body):
    body(Phase(0, z=0))
    body(Phase(1, a=0, z=1))
    body(Phase(2, f=0, a=1, z=2))
    with eng.Fori(0, Phase.ROUNDS) as i:
        body(Phase(3, g=i, f=i + 1, a=i + 2, z=i + 3))
    body(Phase(4, g=NP - 3, f=NP - 2, a=NP - 1))
    body(Phase(5, g=NP - 2, f=NP - 1))
    body(Phase(6, g=NP - 1))


def bass_decoder_layer(nc, x, ctx_in, wq, wk, wv, wo, gamma, beta, xwk, xwv, xbv, xwq, xbq, xwo, xbo,
                       wr, br, w1, b1, w2, b2, out):
    x_v = x.rearrange("b (t p) e -> p (b t) e", p=P)
    out_v = out.rearrange("b (t p) e -> p (b t) e", p=P)
    ctx_v = ctx_in.rearrange("(n b) c e -> (b c) n e", b=2)

    ctx = ExitStack()
    with ctx:
        def sb(name, shape, dt=F32):
            return ctx.enter_context(nc.sbuf_tensor(name, shape, dt))

        def ps(name, shape):
            return ctx.enter_context(nc.psum_tensor(name, shape, F32))

        def sem(name):
            return ctx.enter_context(nc.semaphore(name))

        ident = sb("ident", [P, P])
        ident_bf = sb("ident_bf", [P, P], BF16)
        causal = sb("causal", [P, NG, P], BF16)
        zeros = sb("zeros", [NJ, 1, TOK])
        ones_r = sb("ones_r", [2, P], F32R)
        wT_hi = sb("wT_hi", [P, 4, P], F32R)
        wT_lo = sb("wT_lo", [P, 4, P], F32R)
        xwq_hi = sb("xwq_hi", [P, P], F32R)
        xwq_lo = sb("xwq_lo", [P, P], F32R)
        vec = sb("vec", [P, 4])
        bq_hi = sb("bq_hi", [P, 2], F32R)
        bq_lo = sb("bq_lo", [P, 2], F32R)
        wob = sb("wob", [P, P])
        xbo_b = sb("xbo_b", [P, P])
        br_b = sb("br_b", [P, NE])
        wr_hi = sb("wr_hi", [P, NE], F32R)
        wr_lo = sb("wr_lo", [P, NE], F32R)
        biasT = sb("biasT", [P, CHUNKS + NE])
        w1_hi = sb("w1_hi", [P, NE, F], F32R)
        w1_lo = sb("w1_lo", [P, NE, F], F32R)
        w2_hi = sb("w2_hi", [P, CHUNKS, E], F32R)
        w2_lo = sb("w2_lo", [P, CHUNKS, E], F32R)
        ka_hi = sb("ka_hi", [P, NP * P], F32R)
        ka_lo = sb("ka_lo", [P, NP * P], F32R)
        kc = sb("kc", [2, NP * P], F32R)
        vo_hi = sb("vo_hi", [P, NP, E], F32R)
        vo_lo = sb("vo_lo", [P, NP, E], F32R)
        x_t = sb("x_t", [P, NT, E])
        x_r = sb("x_r", [P, NT, E])
        st6 = sb("st6", [P, NT, 6])
        mv = sb("mv", [P, NT, 2])
        eps_t = sb("eps_t", [P, NT])
        minus_half = sb("minus_half", [P, NT])
        vareps = sb("vareps", [P, NT])
        rstd = sb("rstd", [P, NT])
        ln = sb("ln", [P, NT, E])
        tT_hi = sb("tT_hi", [P, TOK], F32R)
        tT_lo = sb("tT_lo", [P, TOK], F32R)
        qk = sb("qk", [P, 4, TOK], F32R)
        q_hi, q_lo, k_hi, k_lo = (qk[:, n, :] for n in range(4))
        stacks = sb("stacks", [P, 2, NG, TOK], F32R)
        qs, ks = stacks[:, 0], stacks[:, 1]
        v_t = sb("v_t", [P, NT, H, VW])
        negmax = sb("negmax", [P, NT, H])
        nm_hi, nm_lo = q_hi[0:H, :], q_lo[0:H, :]
        prob = sb("prob", [P, 2, NJ, 3 * P])
        attT = sb("attT", [P, 2, NG, S])
        rden = sb("rden", [P, NT, H])
        att = sb("att", [P, NT, E])
        x1 = sb("x1", [P, NT, E])
        vec_rows = x1[0:4, 0, :]
        bias_rows = x1[0:CHUNKS + NE, 1, :]
        wr_in = x1[:, 2, 0:NE]
        woT = x1[:, 3, :]
        x1b = att
        cmax = sb("cmax", [P, NT])
        csum = sb("csum", [P, NT])
        crec = sb("crec", [P, NT])
        cp = sb("cp", [P, NT, P])
        cpT_hi, cpT_lo = tT_hi, tT_lo
        sums = sb("sums", [P, 2, NT, E])
        x2, acc = sums[:, 0], sums[:, 1]
        w_in = sums[:, :, :, :].rearrange("p a k e -> p (a k) e")
        fT_hi = sb("fT_hi", [P, TOK], F32R)
        fT_lo = sb("fT_lo", [P, TOK], F32R)
        xT_hi, xT_lo = ({n: w[:, k * P:(k + 1) * P] for k, n in enumerate(("xwk", "xwv", "xwo"))}
                        for w in (fT_hi, fT_lo))
        hr = sb("hr", [P, RB, TOK])
        h_hi = sb("h_hi", [P, HB, TOK], F32R)
        h_lo = sb("h_lo", [P, HB, TOK], F32R)
        y_sb = sb("y_sb", [P, NE, TOK])
        stage = y_sb
        c_in = hr[:, 0:2, :].rearrange("p b t -> p (b t)").rearrange("p (n e) -> p n e", e=E)
        (cT_hi, kp_hi, vp_hi), (cT_lo, kp_lo, vp_lo) = ([w[:, k, :] for k in range(3)] for w in (h_hi, h_lo))
        kc_lo = cT_lo[0:1, :]
        lgt = sb("lgt", [P, NT, NE])
        lmax = sb("lmax", [P, NT])
        above = sb("above", [P, NT, NE])
        lshift = sb("lshift", [P, NT])
        part = sb("part", [P, NT, NE])
        part2 = sb("part2", [P, NT, NE])
        part4 = sb("part4", [P, NT, 4])
        part8 = sb("part8", [P, NT, 2])
        crec2 = sb("crec2", [P, NT])
        mass = sb("mass", [P, NT])
        shift = sb("shift", [P, NT])
        gate0 = lgt
        gate = sb("gate", [P, NT, NE])
        xs = sb("xs", [P, NT, NE])

        sbuf_s = ps("sbuf_s", [P, NJ, TOK])
        sbuf_m = ps("sbuf_m", [P, TOK])
        h_ps = ps("h_ps", [P, 2, TOK])
        y_ps = ps("y_ps", [P, TOK])
        ps_of = {"s": sbuf_s[:, 0, :], "t": sbuf_s[:, 2, :], "m": sbuf_m[:, :],
                 "u": h_ps[:, 0, :], "v": h_ps[:, 1, :], "y": y_ps[:, :]}
        halves = {"s": sbuf_s[:, 0:2, :], "t": sbuf_s[:, 2:4, :]}

        x_loaded = sem("x_loaded")
        xr_loaded = sem("xr_loaded")
        xr_biased = sem("xr_biased")
        wq_loaded = sem("wq_loaded")
        w_loaded = sem("w_loaded")
        c_loaded = sem("c_loaded")
        w1_loaded = sem("w1_loaded")
        w2_loaded = sem("w2_loaded")
        ident_made = sem("ident_made")
        mask_base = sem("mask_base")
        const_made = sem("const_made")
        set_full = sem("set_full")
        set_hi = sem("set_hi")
        set_free = sem("set_free")
        table_hi = sem("table_hi")
        w1_hi_made = sem("w1_hi_made")
        w1_lo_made = sem("w1_lo_made")
        w2_hi_made = sem("w2_hi_made")
        w2_lo_made = sem("w2_lo_made")
        small_hi = sem("small_hi")
        small_lo = sem("small_lo")
        kc_placed = sem("kc_placed")
        dve_step = sem("dve_step")
        pool_step = sem("pool_step")
        full = {b: sem(f"full_{b}") for b in BUFFERS}
        free = {b: sem(f"free_{b}") for b in BUFFERS}
        var_made = {k: sem(f"var_made_{k}") for k in "za"}
        vareps_made = {k: sem(f"vareps_made_{k}") for k in "za"}
        rstd_made = {k: sem(f"rstd_made_{k}") for k in "za"}
        normed = {k: sem(f"normed_{k}") for k in "za"}
        hi_made = {k: sem(f"hi_made_{k}") for k in "za"}
        stacked = sem("stacked")
        nm_stacked = [sem(f"nm_stacked_{b}") for b in range(2)]
        nm_cleared = sem("nm_cleared")
        pool_turn = sem("pool_turn")
        prob_made = sem("prob_made")
        cmax_made = sem("cmax_made")
        x1b_made = sem("x1b_made")
        h_full = sem("h_full")
        h_free = sem("h_free")
        hr_made = sem("hr_made")
        hlo_made = sem("hlo_made")
        second_done = sem("second_done")
        y_free = sem("y_free")
        above_made = sem("above_made")
        acc_begun = sem("acc_begun")
        gate_turn = sem("gate_turn")
        stored = sem("stored")

        block = ctx.enter_context(nc.Block())

        def filled(eng, ph, step):
            eng.wait_ge(full[step[3]], ph.fill(step) + 1)

        def drained(eng, ph, name, n=0):
            step = ph.find(name, n)
            eng.wait_ge(free[step[3]], ph.fill(step) + 1)

        def words(ap):
            return ap.bitcast(F32)

        def pair_of_heads(n):
            return prob[:, n // 2 % 2, 2 * (n % 2):2 * (n % 2) + 2, :]

        def blocks(ap, first):
            b = ap.rearrange("p (c t) -> p c t", t=P)
            return b[:, 0:3:2, :] if first else b[:, 1, :]

        def as_w2(ap):
            return ap.rearrange("p n f -> p (n f)").rearrange("p (c d) -> p c d", d=E)

        SPLIT = {"T1": ("z", 0, 3), "Q": ("z", 1, 3), "K": ("z", 2, 3),
                 "TA": ("a", 0, 4), "T2": ("a", 1, 4), "PT": ("a", 2, 4), "T3": ("a", 3, 4)}
        SPLIT_BUF = {"T1": (tT_hi, tT_lo), "Q": (q_hi, q_lo), "K": (k_hi, k_lo), "TA": (tT_hi, tT_lo),
                     "T2": (tT_hi, tT_lo), "PT": (cpT_hi, cpT_lo), "T3": (fT_hi, fT_lo)}
        SPLIT_SCALE = {"K": K_SCALE}
        STACK_DMAS = 3 * NG
        SQUARE = {"wo": 3, "xwk": 4, "xwv": 5, "xwo": 6}

        def hi_wait(eng, ph, name):
            k, at, n = SPLIT[name]
            pair = ph.z if k == "z" else ph.a
            eng.wait_ge(hi_made[k], pair * n + at + 1)

        @block.sync
        def _(sp):
            def row(v):
                return v.rearrange("(a e) -> a e", a=1)

            sp.dma_start(x_t[:, :, :], x_v[:, 0:NT, :]).then_inc(x_loaded, 16)
            for n, w in enumerate([wq, wk, wv]):
                sp.dma_start(w_in[:, n, :], w).then_inc(wq_loaded, 16)
            for n, v in enumerate([gamma, beta, xbv, xbq]):
                sp.dma_start(vec_rows[n:n + 1, :], row(v)).then_inc(wq_loaded, 16)
            for n, w in enumerate([wo, xwk, xwv, xwo, xwq]):
                sp.dma_start(w_in[:, 3 + n, :], w).then_inc(w_loaded, 16)
            sp.dma_start(bias_rows[0:CHUNKS, :], b1.rearrange("n (c p) -> (n c) p", p=P)).then_inc(w_loaded, 16)
            sp.dma_start(bias_rows[CHUNKS:CHUNKS + NE, :], b2).then_inc(w_loaded, 16)
            sp.dma_start(wr_in[:, :], wr).then_inc(w_loaded, 16)
            sp.dma_start(xbo_b[:, :], row(xbo).to_broadcast([P, E])).then_inc(w_loaded, 16)
            sp.dma_start(br_b[:, :], row(br).to_broadcast([P, NE])).then_inc(w_loaded, 16)
            sp.dma_start(c_in[:, :, :], ctx_v).then_inc(c_loaded, 16)
            sp.dma_start(stage[:, :, :], w1.rearrange("n d f -> d n f")).then_inc(w1_loaded, 16)
            sp.wait_ge(const_made, 8)

            def stack_rows(ph):
                drained(sp, ph, "K")
                for r, src in enumerate((qk[:, 0:4:2, :], qk[:, 1:3, :], qk[:, 0:4:3, :])):
                    for g in range(NG):
                        sp.dma_start(words(stacks[r:P:4, :, g, :]), words(src[g * 32:(g + 1) * 32, :, :]))\
                          .then_inc(stacked, 16)

            def nm_rows(ph, b):
                drained(sp, ph, "MT", b)
                t = slice(b * S, (b + 1) * S)
                for g in range(NG):
                    for r, src in enumerate((nm_hi, nm_lo)):
                        sp.dma_start(words(qs[3 + 4 * r:P:ROWS, g, t]), words(src[g * NJ:(g + 1) * NJ, t]))\
                          .then_inc(nm_stacked[b], 16)

            def step(ph, s):
                name, n = s[1:3]
                if name == "V":
                    stack_rows(ph)
                if name == "MT":
                    nm_rows(ph, n)
                if (name, n) == ("SC", 15):
                    filled(sp, ph, s)
                    for r in range(2):
                        sp.dma_start(words(qs[3 + 4 * r:P:ROWS, :, :]), zeros[:, :, :].to_broadcast([NJ, NG, TOK]))\
                          .then_inc(nm_cleared, 16)
                if (name, n) == ("GA", NE // 2 - 1):
                    drained(sp, ph, name, n)
                    sp.dma_start(out_v[:, bass.ts(ph.g, NT), :], acc).then_inc(stored, 16)
                if name == "kc":
                    drained(sp, ph, name, n)
                    sp.dma_start(words(kc[1:2, n * TOK:(n + 1) * TOK]), words(kc_lo)).then_inc(kc_placed, 16)
                if (name, n) == ("vo", 1):
                    sp.wait_ge(w1_hi_made, 4)
                    sp.wait_ge(w1_lo_made, 4)
                    sp.dma_start(as_w2(stage[:, :, :]), w2.rearrange("n (c p) d -> p (n c) d", p=P)).then_inc(w2_loaded, 16)

            def body(ph):
                if "Z" in ph.parts and ph.a is not None:
                    sp.wait_ge(normed["z"], ph.z)
                    sp.dma_start(x_t[:, :, :], x_v[:, bass.ts(ph.z, NT), :]).then_inc(x_loaded, 16)
                if "A" in ph.parts:
                    if ph.f is not None:
                        sp.wait_ge(free["m"], ph.before["m"])
                    sp.dma_start(x_r[:, :, :], x_v[:, bass.ts(ph.a, NT), :]).then_inc(xr_loaded, 16)
                for t in range(SLOTS):
                    for s in ph.steps(t):
                        step(ph, s)

            run_phases(sp, body)
            sp.wait_ge(nm_cleared, 32 * NP)
            sp.wait_ge(stored, 16 * NP + 16)

        @block.gpsimd
        def _(pool):
            pool.memset(ident[:, :], 0.0).then_inc(ident_made, 1)
            pool.wait_ge(ident_made, 1)
            pool.affine_select(out=ident[:, :], in_=ident[:, :], compare_op=ALU.not_equal, fill=1.0, base=0,
                               pattern=[[-1, P]], channel_multiplier=1).then_inc(ident_made, 1)
            pool.memset(eps_t[:, :], LN_EPS).then_inc(mask_base, 1)
            pool.memset(minus_half[:, :], -0.5).then_inc(mask_base, 1)
            pool.wait_ge(mask_base, 2)
            steps_done = [0]

            def mark(ins):
                steps_done[0] += 1
                ins.then_inc(pool_step, 1)

            def settle():
                pool.wait_ge(pool_step, steps_done[0])

            def masks():
                pool.memset(words(qs[:, :, :]), 0.0).then_inc(const_made, 1)
                pool.memset(words(ks[:, :, :]), 1.0).then_inc(const_made, 1)
                pool.memset(v_t[:, :, :, :], 0.0).then_inc(mask_base, 1)
                pool.memset(causal[:, :, :], 0.0).then_inc(mask_base, 1)
                pool.wait_ge(mask_base, 4)
                pool.memset(v_t[:, :, :, D:D + 1], 1.0).then_inc(const_made, 1)
                pool.tensor_copy(ident_bf[:, :], ident[:, :]).then_inc(const_made, 1)
                pool.affine_select(out=causal[:, :, :], in_=causal[:, :, :], compare_op=ALU.is_ge, fill=MASKED,
                                   base=0, pattern=[[0, NG], [-1, P]], channel_multiplier=1).then_inc(const_made, 1)
                pool.memset(cp[:, :, :], 0.0).then_inc(const_made, 1)
                pool.memset(zeros[:, :, :], 0.0).then_inc(const_made, 1)
                pool.memset(words(ones_r[:, :]), 1.0).then_inc(const_made, 1)

            def mask(ph, s):
                drained(pool, ph, "SC", s[2])
                pool.sem_inc(pool_turn, 1)
                v = pair_of_heads(s[2])[:, :, 0:2 * P]
                pool.affine_select(out=v, in_=v, compare_op=ALU.is_ge, fill=0.0, base=0,
                                   pattern=[[0, 2], [0, 2], [1, P]], channel_multiplier=-1).then_inc(prob_made, 1)

            def inverse_deviation(k, at):
                pool.wait_ge(var_made[k], at * NT + NT)
                pool.tensor_tensor(vareps[:, :], mv[:, :, 1], eps_t[:, :], ALU.add).then_inc(vareps_made[k], 1)
                pool.wait_ge(vareps_made[k], at + 1)
                pool.tensor_tensor(rstd[:, :], vareps[:, :], minus_half[:, :], ALU.pow).then_inc(rstd_made[k], 1)

            def bisect(it):
                width = WIDTH * 0.5 ** (it + 1)
                settle()
                mark(pool.tensor_scalar(part[:, :, :], above[:, :, :], width, 0.0, ALU.subtract, ALU.max))
                settle()
                mark(pool.tensor_tensor(part2[:, :, :], part[:, :, :], part[:, :, :], ALU.mult))
                settle()
                mark(pool.tensor_tensor(part4[:, :, :], part2[:, :, 0:4], part2[:, :, 4:8], ALU.add))
                settle()
                mark(pool.tensor_tensor(part8[:, :, :], part4[:, :, 0:2], part4[:, :, 2:4], ALU.add))
                settle()
                mark(pool.tensor_tensor(mass[:, :], part8[:, :, 0], part8[:, :, 1], ALU.add))
                settle()
                if it < BISECTIONS - 1:
                    mark(pool.tensor_scalar(shift[:, :], mass[:, :], 1.0, width, ALU.is_ge, ALU.mult))
                    settle()
                    mark(pool.tensor_tensor(above[:, :, :], above[:, :, :],
                                            shift[:, :].unsqueeze(2).to_broadcast([P, NT, NE]), ALU.subtract))
                else:
                    pool.sem_inc(gate_turn, 1)

            def step(ph, s):
                name, n = s[1:3]
                if name == "SC":
                    mask(ph, s)
                if (name, n) == ("BT", 3):
                    inverse_deviation("a", ph.a * 3)
                if name == "XR":
                    pool.wait_ge(xr_loaded, ph.a * 16 + 16)
                    pool.tensor_tensor(x_r[:, :, :], x_r[:, :, :], wob[:, :].unsqueeze(1).to_broadcast([P, NT, E]),
                                       ALU.add).then_inc(xr_biased, 1)
                if name == "WO":
                    inverse_deviation("a", ph.a * 3 + 1)
                    drained(pool, ph, "WO")
                    pool.tensor_tensor(x1b[:, :, :], x1[:, :, :], xbo_b[:, :].unsqueeze(1).to_broadcast([P, NT, E]),
                                       ALU.add).then_inc(x1b_made, 1)
                if name == "XO":
                    inverse_deviation("a", ph.a * 3 + 2)

            def body(ph):
                if "W" in ph.parts:
                    inverse_deviation("z", ph.z)
                    masks()
                    for q in range(4):
                        e = slice(2 * q, 2 * q + 2)
                        pool.wait_ge(w1_hi_made, q + 1)
                        pool.tensor_tensor(w1_lo[:, e, :], stage[:, e, :], w1_hi[:, e, :], ALU.subtract)\
                            .then_inc(w1_lo_made, 1)
                    for n in range(EARLY):
                        mask(ph, ph.find("SC", n))
                    return
                for t in range(SLOTS):
                    if "Z" in ph.parts and t == ph.ln_z:
                        inverse_deviation("z", ph.z)
                    if "X" in ph.parts:
                        if t == 1:
                            pool.wait_ge(above_made, ph.f + 1)
                            pool.sem_inc(pool_turn, 1)
                        if t == SUM_AT:
                            pool.wait_ge(stored, ph.f * 16 + 16)
                            pool.sem_inc(pool_turn, 1)
                            pool.tensor_copy(acc, x2).then_inc(acc_begun, 1)
                        if BISECT_FROM <= t < BISECT_FROM + BISECTIONS:
                            bisect(t - BISECT_FROM)
                    for s in ph.steps(t):
                        step(ph, s)
                    for q in range(4):
                        c = slice(8 * q, 8 * q + 8)
                        if ph.once and t == W2_AT[q]:
                            pool.wait_ge(w2_hi_made, q + 1)
                            pool.tensor_tensor(w2_lo[:, c, :], as_w2(stage[:, :, :])[:, c, :], w2_hi[:, c, :],
                                               ALU.subtract).then_inc(w2_lo_made, 1)
                settle()
                pool.sem_inc(pool_turn, 1)
                pool.sem_clear(pool_step)
                steps_done[0] = 0

            run_phases(pool, body)

        @block.tensor
        def _(pe):
            def three(out_ap, w_hi, w_lo, m_hi, m_lo, start=True, stop=True):
                pe.matmul(out_ap, w_hi, m_lo, start=start, stop=False)
                pe.matmul(out_ap, w_lo, m_hi, start=False, stop=False)
                return pe.matmul(out_ap, w_hi, m_hi, start=False, stop=stop)

            pe.wait_ge(ident_made, 2)
            pe.wait_ge(wq_loaded, 16 * 7)
            for n in range(3):
                pe.transpose(sbuf_s[:, n, 0:P], w_in[:, n, :], ident[:, :])
            pe.transpose(sbuf_s[:, 3, 0:4], vec_rows[:, :], ident[0:4, 0:4]).then_inc(set_full, 1)
            pe.wait_ge(set_free, 1)

            def transposes(dst, src):
                for k in range(NT):
                    last = pe.transpose(dst[:, k * P:(k + 1) * P], src[:, k, :], ident[:, :])
                return last

            def project_rows(dst, t_hi, t_lo, w_hi, w_lo):
                for k in range(NT):
                    w = slice(k * P, (k + 1) * P)
                    last = three(dst[:, w], t_hi[:, w], t_lo[:, w], w_hi, w_lo)
                return last

            def max_scores(ph, n, dst):
                b, kind = divmod(n // 2, 3)
                tile = 2 * b + (kind > 0)
                if n == 0:
                    pe.wait_ge(stacked, (ph.z + 1) * 16 * STACK_DMAS)
                    if ph.a is not None:
                        pe.wait_ge(nm_cleared, ph.z * 32)
                    else:
                        pe.wait_ge(const_made, 8)
                gs, width = (range(NG), P) if kind == 0 else (range(2 * kind - 2, 2 * kind), S)
                for at, g in enumerate(gs):
                    for j in range(2):
                        r = slice(ROWS * (2 * (n % 2) + j), ROWS * (2 * (n % 2) + j + 1))
                        pe.matmul(dst[:, j, at * width:(at + 1) * width],
                                  qs[r, g, tile * P:(tile + 1) * P], ks[r, g, b * S:b * S + width],
                                  start=(at == 0), stop=True, skip_group_check=(at > 0))
                for j in range(2):
                    diagonal = dst[:, j, :].rearrange("p (g s) -> p g s", s=width)[:, :, width - P:width]
                    last = pe.matmul(diagonal, ident_bf[:, :], causal[:, 0:len(gs), :],
                                     start=False, stop=True, skip_group_check=True)
                return last

            def scores(ph, n, dst):
                b, g = divmod(n // 2, NG)
                if n % 8 == 0:
                    pair = ph.z if n < EARLY else ph.a
                    pe.wait_ge(nm_stacked[b], pair * 128 + 128)
                for first in (True, False):
                    for j in range(2):
                        r = slice(ROWS * (2 * (n % 2) + j), ROWS * (2 * (n % 2) + j + 1))
                        k0, q0, w = (0, 0, S) if first else (P, P, P)
                        last = pe.matmul(blocks(dst[:, j, 0:3 * P], first), ks[r, g, b * S + k0:b * S + k0 + P],
                                         qs[r, g, b * S + q0:b * S + q0 + w], start=True, stop=True)
                return last

            def values(ph, n, dst):
                b, g = divmod(n, NG)
                pe.wait_ge(prob_made, ph.a * 16 + 2 * n + 2)
                for first in (True, False):
                    for j in range(NJ):
                        o = dst[VW * j:VW * (j + 1), :]
                        last = pe.matmul(o[:, 0:S] if first else o[:, P:S], v_t[:, 2 * b + (not first), g * NJ + j, :],
                                         blocks(prob[:, n % 2, j, :], first), start=first, stop=True,
                                         skip_group_check=not first)
                return last

            def step(ph, s):
                t, name, n, buf = s
                if buf == NO_BUFFER:
                    return
                before = ph.fill(s)
                if not (isinstance(before, int) and before == 0):
                    pe.wait_ge(free[buf], before)
                dst = ps_of[buf]
                if name == "T1":
                    pe.wait_ge(normed["z"], ph.z + 1)
                    last = transposes(dst, ln)
                if name in ("TA", "T2", "T3"):
                    pe.wait_ge(normed["a"], ph.a * 3 + ("TA", "T2", "T3").index(name) + 1)
                    last = transposes(dst, ln)
                if name in ("Q", "K"):
                    drained(pe, ph, "T1")
                    w = "QK".index(name)
                    last = three(dst, wT_hi[:, w, :], wT_lo[:, w, :], tT_hi[:, :], tT_lo[:, :])
                if name == "V":
                    last = project_rows(dst, tT_hi, tT_lo, wT_hi[:, 2, :], wT_lo[:, 2, :])
                if name == "MAX":
                    last = max_scores(ph, n, halves[buf])
                if name == "MT":
                    drained(pe, ph, "MAX", 6 * n + 4)
                    drained(pe, ph, "MAX", 6 * n + 5)
                    for k in range(2 * n, 2 * n + 2):
                        last = pe.transpose(dst[0:H, k * P:(k + 1) * P], negmax[:, k, :], ident[:, :])
                if name == "SC":
                    last = scores(ph, n, halves[buf])
                if name == "PV":
                    last = values(ph, n, dst)
                if name == "BT":
                    b, k = divmod(n, 2)
                    if ph.find("PV", 4 * b + 2)[3] != ph.find("PV", 4 * b + 3)[3]:
                        drained(pe, ph, "PV", 4 * b + 2)
                    drained(pe, ph, "PV", 4 * b + 3)
                    for g in range(NG):
                        last = pe.transpose(dst[:, g * P:(g + 1) * P], attT[:, b, g, k * P:(k + 1) * P], ident[:, :])
                if name == "WO":
                    drained(pe, ph, "TA")
                    last = project_rows(dst, tT_hi, tT_lo, wT_hi[:, 3, :], wT_lo[:, 3, :])
                if name == "XS":
                    drained(pe, ph, "T2")
                    if ph.once:
                        pe.wait_ge(kc_placed, 32)
                    for k in range(NT):
                        w = slice(k * P, (k + 1) * P)
                        c = bass.ds(ph.a * P + (k // 2) * C, C)
                        o = dst[:, k * C:(k + 1) * C]
                        three(o, tT_hi[:, w], tT_lo[:, w], ka_hi[:, c], ka_lo[:, c], stop=False)
                        last = pe.matmul(o, ones_r[:, :], kc[:, c], start=False, stop=True)
                if name == "PT":
                    drained(pe, ph, "XS")
                    last = transposes(dst, cp)
                if name == "XO":
                    drained(pe, ph, "PT")
                    for k in range(NT):
                        w = slice(k * P, (k + 1) * P)
                        v = bass.ds(ph.a, 1)
                        last = three(dst[:, w], cpT_hi[:, w], cpT_lo[:, w], vo_hi[:, v, :], vo_lo[:, v, :])
                if name == "LG":
                    for k in range(NT):
                        w = slice(k * P, (k + 1) * P)
                        last = three(dst[:, k * NE:(k + 1) * NE], fT_hi[:, w], fT_lo[:, w], wr_hi[:, :], wr_lo[:, :])
                if name == "GA":
                    pe.wait_ge(y_free, ph.g * NE + NE)
                    for e in range(2):
                        for k in range(NT):
                            w = slice(k * P, (k + 1) * P)
                            last = pe.transpose(halves[buf][:, e, w], y_sb[:, 2 * n + e, w], ident[:, :])
                if (name, n) == ("wo", 0):
                    pe.wait_ge(w_loaded, 16 * 10)
                if name in SQUARE:
                    last = pe.transpose(dst[:, 0:P], w_in[:, SQUARE[name], :], ident[:, :])
                if name == "bias":
                    last = pe.transpose(dst[:, 0:CHUNKS + NE], bias_rows[:, :], ident[0:CHUNKS + NE, 0:CHUNKS + NE])
                if name == "bo":
                    drained(pe, ph, "wo")
                    last = pe.matmul(dst[:, 0:E], vec[:, 1:2].to_broadcast([P, P]), woT, start=True, stop=True)
                if name == "cT":
                    pe.wait_ge(c_loaded, 16)
                    last = transposes(dst, c_in[:, n * NT:(n + 1) * NT, :])
                if name in ("kp", "vp"):
                    w = "xw" + name[0]
                    drained(pe, ph, "cT", n)
                    last = three(dst, xT_hi[w], xT_lo[w], cT_hi, cT_lo)
                if name == "ka":
                    drained(pe, ph, "vp", n)
                    pe.wait_ge(small_lo, 2)
                    last = three(dst, xwq_hi[:, :], xwq_lo[:, :], kp_hi, kp_lo)
                if name == "kc":
                    last = three(dst[0:2, :], bq_hi[:, :], bq_lo[:, :], kp_hi, kp_lo)
                if name == "vo":
                    last = project_rows(dst, vp_hi, vp_lo, xT_hi["xwo"], xT_lo["xwo"])
                last.then_inc(full[buf], 1)

            def first_product(ph, c):
                e, fb = divmod(c, FB)
                if c == 0:
                    pe.wait_ge(free["m"], ph.before["m"])
                    for b in "uvy":
                        pe.wait_ge(free[b], ph.before[b])
                    pe.wait_ge(w1_lo_made, 4)
                    pe.wait_ge(w2_lo_made, 4)
                if 2 <= c < DVE_BLOCKS + 2:
                    pe.wait_ge(hr_made, ph.f * DVE_BLOCKS + c - 1)
                if c >= DVE_BLOCKS + 2:
                    pe.wait_ge(h_free, ph.f * CHUNKS + c - 1)
                w = slice(fb * P, (fb + 1) * P)
                three(h_ps[:, c % 2, :], w1_hi[:, e, w], w1_lo[:, e, w], fT_hi[:, :], fT_lo[:, :]).then_inc(h_full, 1)

            def second_product(ph, c):
                e, fb = divmod(c, FB)
                pe.wait_ge(hlo_made, ph.f * CHUNKS + c + 1)
                if fb == 0 and e > 0:
                    pe.wait_ge(y_free, ph.f * NE + e)
                three(y_ps[:, :], w2_hi[:, c, :], w2_lo[:, c, :], h_hi[:, c % HB, :], h_lo[:, c % HB, :],
                      start=(fb == 0), stop=(fb == FB - 1)).then_inc(second_done, 1)

            def body(ph):
                for t in range(SLOTS):
                    if "X" in ph.parts and t < CHUNKS:
                        first_product(ph, t)
                    if "X" in ph.parts and 0 <= t - LAG < CHUNKS:
                        second_product(ph, t - LAG)
                    for s in ph.steps(t):
                        step(ph, s)

            run_phases(pe, body)

        @block.scalar
        def _(act):
            act.wait_ge(set_full, 1)
            act.activation(wT_hi[:, 0:2, :], sbuf_s[:, 0:2, 0:P], ACT.Copy)
            act.activation(wT_hi[:, 2, :].rearrange("p (h d) -> p h d", d=D),
                           sbuf_s[:, 2, 0:P].rearrange("p (d h) -> p h d", h=H), ACT.Copy)
            act.activation(vec[:, :], sbuf_s[:, 3, 0:4], ACT.Copy).then_inc(set_hi, 1)

            def table(ph, s):
                t, name, n, buf = s
                filled(act, ph, s)
                src = ps_of[buf]
                half = slice(n * TOK, (n + 1) * TOK)
                if name == "wo":
                    act.activation(woT, src[:, 0:P], ACT.Copy)
                    ins = act.activation(wT_hi[:, 3, :], src[:, 0:P], ACT.Copy, scale=vec[:, 0:1])
                if name in xT_hi:
                    ins = act.activation(xT_hi[name], src[:, 0:P], ACT.Copy)
                if name == "bo":
                    act.activation(wob[:, :], src[:, 0:E], ACT.Copy).then_inc(free[buf], 1)
                    return
                if name == "bias":
                    act.activation(biasT[:, :], src[:, 0:CHUNKS + NE], ACT.Copy).then_inc(free[buf], 1)
                    return
                if name in ("cT", "kp"):
                    if (name, n) == ("cT", 1):
                        act.wait_ge(kc_placed, 16)
                    ins = act.activation(cT_hi if name == "cT" else kp_hi, src, ACT.Copy)
                if name == "vp":
                    ins = act.activation(vp_hi, src, ACT.Identity, bias=vec[:, 2:3])
                if name == "ka":
                    ins = act.activation(ka_hi[:, half], src, ACT.Copy, scale=C_SCALE)
                if name == "kc":
                    ins = act.activation(kc[0:1, half], src[0:1, :], ACT.Copy, scale=C_SCALE)
                if name == "vo":
                    ins = act.activation(vo_hi[:, n * NT:(n + 1) * NT, :], src.rearrange("p (n e) -> p n e", e=E), ACT.Copy)
                ins.then_inc(table_hi, 1)

            def step(ph, s):
                t, name, n, buf = s
                if (name, n) in W_ORDER:
                    table(ph, s)
                if name in SPLIT:
                    filled(act, ph, s)
                    if name == "Q" and ph.a is not None:
                        act.wait_ge(stacked, ph.z * 16 * STACK_DMAS)
                    act.activation(SPLIT_BUF[name][0][:, :], ps_of[buf], ACT.Copy,
                                   scale=SPLIT_SCALE.get(name, 1.0)).then_inc(hi_made[SPLIT[name][0]], 1)
                if name == "SC":
                    filled(act, ph, s)
                    if n >= 4:
                        filled(act, ph, ph.find("PV", n // 2 - 2))
                    act.activation(pair_of_heads(n), halves[buf][:, :, 0:3 * P], ACT.Exp).then_inc(free[buf], 1)
                if name == "PV":
                    filled(act, ph, s)
                    act.activation(attT[:, n // NG, n % NG, :], ps_of[buf][:, 0:S], ACT.Copy).then_inc(free[buf], 1)
                if name == "XS":
                    act.wait_ge(cmax_made, ph.a + 1)
                    for k in range(NT):
                        h0 = (k // 2) * C
                        last = act.activation(cp[:, k, h0:h0 + C], ps_of[buf][:, k * C:(k + 1) * C], ACT.Exp,
                                              bias=cmax[:, k:k + 1], accum_out=csum[:, k:k + 1])
                    last.then_inc(free[buf], 1)

            def hidden(ph, c):
                bias = biasT[:, c:c + 1]
                if c >= DVE_BLOCKS:
                    act.wait_ge(h_full, ph.f * CHUNKS + c + 1)
                    act.wait_ge(hlo_made, ph.f * CHUNKS + c - RB + 1)
                    act.activation(hr[:, c % RB, :], h_ps[:, c % 2, :], ACT.Relu, bias=bias)
                if c >= HB:
                    act.wait_ge(second_done, ph.f * CHUNKS + c - HB + 1)
                if c >= DVE_BLOCKS:
                    act.activation(h_hi[:, c % HB, :], h_ps[:, c % 2, :], ACT.Relu, bias=bias).then_inc(h_free, 1)
                else:
                    act.wait_ge(hr_made, ph.f * DVE_BLOCKS + c + 1)
                    act.activation(h_hi[:, c % HB, :], hr[:, c % RB, :], ACT.Copy).then_inc(h_free, 1)

            def evacuate_y(ph, e):
                if "G" in ph.parts and e % 2 == 0:
                    filled(act, ph, ph.find("GA", e // 2))
                act.wait_ge(second_done, ph.f * CHUNKS + FB * (e + 1))
                act.activation(y_sb[:, e, :], y_ps[:, :], ACT.Identity,
                               bias=biasT[:, CHUNKS + e:CHUNKS + e + 1]).then_inc(y_free, 1)

            def body(ph):
                for t in range(SLOTS):
                    if "X" in ph.parts and t < CHUNKS:
                        hidden(ph, t)
                    c = t - LAG
                    if "X" in ph.parts and 0 <= c < CHUNKS and c % FB == FB - 1:
                        evacuate_y(ph, c // FB)
                    for s in ph.steps(t):
                        step(ph, s)
                    if "W" in ph.parts and t == 4:
                        act.wait_ge(w_loaded, 16 * 10)
                        act.activation(xwq_hi[:, :], w_in[:, 7, :], ACT.Copy)
                        act.activation(wr_hi[:, :], wr_in[:, :], ACT.Copy).then_inc(small_hi, 1)
                    for q in range(4):
                        e, c = slice(2 * q, 2 * q + 2), slice(8 * q, 8 * q + 8)
                        if "W" in ph.parts and t == W1_AT[q]:
                            act.wait_ge(w1_loaded, 16)
                            act.activation(w1_hi[:, e, :], stage[:, e, :], ACT.Copy).then_inc(w1_hi_made, 1)
                        if ph.once and "A" in ph.parts and t == W2_AT[q]:
                            act.wait_ge(w2_loaded, 16)
                            act.activation(w2_hi[:, c, :], as_w2(stage[:, :, :])[:, c, :], ACT.Copy)\
                               .then_inc(w2_hi_made, 1)

            run_phases(act, body)

        @block.vector
        def _(dve):
            steps_done = [0]

            def mark(ins):
                steps_done[0] += 1
                ins.then_inc(dve_step, 1)

            def settle():
                dve.wait_ge(dve_step, steps_done[0])

            dve.sem_inc(stored, 16)

            def setup():
                dve.wait_ge(set_hi, 1)
                dve.tensor_tensor(wT_lo[:, 0:2, :], sbuf_s[:, 0:2, 0:P], wT_hi[:, 0:2, :], ALU.subtract)
                dve.tensor_tensor(wT_lo[:, 2, :].rearrange("p (h d) -> p h d", d=D),
                                  sbuf_s[:, 2, 0:P].rearrange("p (d h) -> p h d", h=H),
                                  wT_hi[:, 2, :].rearrange("p (h d) -> p h d", d=D), ALU.subtract).then_inc(set_free, 1)
                mark(dve.tensor_copy(bq_hi[:, 0:1], vec[:, 3:4]))
                mark(dve.tensor_copy(bq_hi[:, 1:2], vec[:, 3:4]))
                settle()
                dve.tensor_tensor(bq_lo[:, 0:1], vec[:, 3:4], bq_hi[:, 0:1], ALU.subtract)
                dve.tensor_tensor(bq_lo[:, 1:2], vec[:, 3:4], bq_hi[:, 0:1], ALU.subtract).then_inc(small_lo, 0 + 1)

            def table(ph, s):
                t, name, n, buf = s
                if name in ("bias", "bo"):
                    return
                dve.wait_ge(table_hi, [w for w in W_ORDER if w[0] not in ("bias", "bo")].index((name, n)) + 1)
                src = ps_of[buf]
                half = slice(n * TOK, (n + 1) * TOK)
                if name == "wo":
                    ins = dve.scalar_tensor_tensor(out=wT_lo[:, 3, :], in0=src[:, 0:P], scalar=vec[:, 0:1],
                                                   in1=wT_hi[:, 3, :], op0=ALU.mult, op1=ALU.subtract)
                if name in xT_hi:
                    ins = dve.tensor_tensor(xT_lo[name], src[:, 0:P], xT_hi[name], ALU.subtract)
                if name == "cT":
                    ins = dve.tensor_tensor(cT_lo, src, cT_hi, ALU.subtract)
                if name == "kp":
                    ins = dve.tensor_tensor(kp_lo, src, kp_hi, ALU.subtract)
                if name == "vp":
                    ins = dve.scalar_tensor_tensor(out=vp_lo, in0=src, scalar=vec[:, 2:3], in1=vp_hi,
                                                   op0=ALU.add, op1=ALU.subtract)
                if name == "ka":
                    ins = dve.scalar_tensor_tensor(out=ka_lo[:, half], in0=src, scalar=C_SCALE,
                                                   in1=ka_hi[:, half], op0=ALU.mult, op1=ALU.subtract)
                if name == "kc":
                    ins = dve.scalar_tensor_tensor(out=kc_lo, in0=src[0:1, :], scalar=C_SCALE,
                                                   in1=kc[0:1, half], op0=ALU.mult, op1=ALU.subtract)
                if name == "vo":
                    ins = dve.tensor_tensor(vo_lo[:, n * NT:(n + 1) * NT, :], src.rearrange("p (n e) -> p n e", e=E),
                                            vo_hi[:, n * NT:(n + 1) * NT, :], ALU.subtract)
                ins.then_inc(free[buf], 1)

            def statistics(k, src):
                for n in range(NT):
                    mark(dve.bn_stats(st6[:, n, :], src[:, n, :]))
                settle()
                for n in range(NT):
                    dve.bn_aggr(mv[:, n, :], st6[:, n, :]).then_inc(var_made[k], 1)

            def normalise(k, at, src):
                dve.wait_ge(rstd_made[k], at + 1)
                for n in range(NT):
                    ins = dve.tensor_scalar(ln[:, n, :], src[:, n, :], mv[:, n, 0:1], rstd[:, n:n + 1],
                                            ALU.subtract, ALU.mult)
                ins.then_inc(normed[k], 1)

            def step(ph, s):
                t, name, n, buf = s
                src = None if buf == NO_BUFFER else ps_of[buf]
                if (name, n) in W_ORDER:
                    table(ph, s)
                if name in SPLIT:
                    hi, lo = SPLIT_BUF[name]
                    hi_wait(dve, ph, name)
                    if name in SPLIT_SCALE:
                        ins = dve.scalar_tensor_tensor(out=lo[:, :], in0=src, scalar=SPLIT_SCALE[name], in1=hi[:, :],
                                                       op0=ALU.mult, op1=ALU.subtract)
                    else:
                        ins = dve.tensor_tensor(lo[:, :], src, hi[:, :], ALU.subtract)
                    ins.then_inc(free[buf], 1)
                if name == "PT":
                    drained(dve, ph, "XS")
                    mark(dve.reciprocal(crec[:, :], csum[:, :]))
                if name == "V":
                    filled(dve, ph, s)
                    if ph.a is None:
                        dve.wait_ge(const_made, 8)
                    dve.tensor_copy(v_t[:, :, :, 0:D], src.rearrange("p (k h d) -> p k h d", h=H, d=D))\
                       .then_inc(free[buf], 1)
                if name == "MAX":
                    filled(dve, ph, s)
                    b, kind = divmod(n // 2, 3)
                    tile = 2 * b + (kind > 0)
                    heads = slice(0, H) if kind == 0 else slice(8 * (kind - 1), 8 * kind)
                    j = 2 * (n % 2)
                    dve.tensor_reduce(negmax[:, tile, heads].rearrange("p (g j) -> p j g", j=NJ)[:, j:j + 2, :],
                                      halves[buf].rearrange("p j (g s) -> p j g s", g=NG if kind == 0 else 2),
                                      AX.X, ALU.max, negate=True).then_inc(free[buf], 1)
                if name == "MT":
                    filled(dve, ph, s)
                    w = slice(n * S, (n + 1) * S)
                    mark(dve.tensor_copy(nm_hi[:, w], src[0:H, w]))
                    settle()
                    dve.tensor_tensor(nm_lo[:, w], src[0:H, w], nm_hi[:, w], ALU.subtract).then_inc(free[buf], 1)
                if name == "BT":
                    filled(dve, ph, s)
                    v = src.rearrange("p (h w) -> p h w", w=VW)
                    mark(dve.reciprocal(rden[:, n, :], v[:, :, D]))
                    settle()
                    dve.tensor_tensor(att[:, n, :].rearrange("p (h d) -> p h d", d=D), v[:, :, 0:D],
                                      rden[:, n, :].unsqueeze(2).to_broadcast([P, H, D]), ALU.mult).then_inc(free[buf], 1)
                    if n == 3:
                        drained(dve, ph, "BT", 3)
                        statistics("a", att)
                if name == "NZ":
                    normalise("z", ph.z, x_t)
                if name == "NA":
                    normalise("a", ph.a * 3 + n, (att, x1, x2)[n])
                if name == "WO":
                    filled(dve, ph, s)
                    dve.wait_ge(xr_biased, ph.a + 1)
                    dve.tensor_tensor(x1[:, :, :], x_r[:, :, :], src.rearrange("p (k e) -> p k e", e=E),
                                      ALU.add).then_inc(free[buf], 1)
                    drained(dve, ph, "WO")
                    statistics("a", x1)
                if name == "XS":
                    filled(dve, ph, s)
                    dve.tensor_reduce(cmax[:, :], src[:, 0:NT * C].rearrange("p (k c) -> p k c", c=C), AX.X,
                                      ALU.max, negate=True).then_inc(cmax_made, 1)
                if name == "XO":
                    settle()
                    filled(dve, ph, s)
                    dve.wait_ge(x1b_made, ph.a + 1)
                    if ph.f is not None:
                        dve.wait_ge(acc_begun, ph.f + 1)
                    for k in range(NT):
                        ins = dve.scalar_tensor_tensor(out=x2[:, k, :], in0=src[:, k * E:(k + 1) * E],
                                                       scalar=crec[:, k:k + 1], in1=x1b[:, k, :],
                                                       op0=ALU.mult, op1=ALU.add)
                    ins.then_inc(free[buf], 1)
                    drained(dve, ph, "XO")
                    statistics("a", x2)
                if name == "LG":
                    filled(dve, ph, s)
                    dve.tensor_tensor(lgt[:, :, :], src[:, 0:NT * NE].rearrange("p (k e) -> p k e", e=NE),
                                      br_b[:, :].unsqueeze(1).to_broadcast([P, NT, NE]), ALU.add).then_inc(free[buf], 1)
                    drained(dve, ph, "LG")
                    mark(dve.tensor_scalar(xs[:, :, :], lgt[:, :, :], 0.5, None, ALU.mult))
                    settle()
                    mark(dve.tensor_reduce(lmax[:, :], xs[:, :, :], AX.X, ALU.max))
                    settle()
                    mark(dve.tensor_scalar(lshift[:, :], lmax[:, :], -1.0, None, ALU.add))
                    settle()
                    dve.tensor_tensor(above[:, :, :], xs[:, :, :],
                                      lshift[:, :].unsqueeze(2).to_broadcast([P, NT, NE]), ALU.subtract)\
                       .then_inc(above_made, 1)
                if name == "GT":
                    gates(ph)
                if name == "GA":
                    if n == 0:
                        dve.wait_ge(acc_begun, ph.g + 1)
                    else:
                        drained(dve, ph, "GA", n - 1)
                    filled(dve, ph, s)
                    for e in range(2):
                        for k in range(NT):
                            ins = dve.scalar_tensor_tensor(out=acc[:, k, :], in0=halves[buf][:, e, k * E:(k + 1) * E],
                                                           scalar=gate[:, k, 2 * n + e:2 * n + e + 1],
                                                           in1=acc[:, k, :], op0=ALU.mult, op1=ALU.add)
                        if e == 0:
                            mark(ins)
                            settle()
                    ins.then_inc(free[buf], 1)

            def gates(ph):
                dve.wait_ge(gate_turn, ph.f + 1)
                mark(dve.reciprocal(crec2[:, :], mass[:, :]))
                settle()
                mark(dve.tensor_tensor(gate0[:, :, :], part2[:, :, :],
                                       crec2[:, :].unsqueeze(2).to_broadcast([P, NT, NE]), ALU.mult))
                settle()
                mark(dve.scalar_tensor_tensor(out=gate[:, :, :], in0=gate0[:, :, :], scalar=1e-9,
                                              in1=gate0[:, :, :], op0=ALU.is_gt, op1=ALU.mult))

            def hidden_relu(ph, c):
                if c >= RB:
                    dve.wait_ge(hlo_made, ph.f * CHUNKS + c - RB + 1)
                dve.wait_ge(h_full, ph.f * CHUNKS + c + 1)
                dve.tensor_scalar(hr[:, c % RB, :], h_ps[:, c % 2, :], biasT[:, c:c + 1], 0.0, ALU.add, ALU.max)\
                   .then_inc(hr_made, 1)

            def hidden_lo(ph, c):
                dve.wait_ge(h_free, ph.f * CHUNKS + c + 1)
                dve.tensor_tensor(h_lo[:, c % HB, :], hr[:, c % RB, :], h_hi[:, c % HB, :], ALU.subtract)\
                   .then_inc(hlo_made, 1)

            def body(ph):
                for t in range(SLOTS):
                    if "X" in ph.parts and t < CHUNKS:
                        if t < DVE_BLOCKS:
                            hidden_relu(ph, t)
                        if 0 < t <= DVE_BLOCKS:
                            hidden_lo(ph, t - 1)
                        if t >= DVE_BLOCKS:
                            hidden_lo(ph, t)
                    if "Z" in ph.parts and t == ph.ln_z:
                        dve.wait_ge(x_loaded, ph.z * 16 + 16)
                        statistics("z", x_t)
                        if ph.a is None:
                            setup()
                    for s in ph.steps(t):
                        step(ph, s)
                    if "W" in ph.parts and t == 4:
                        dve.wait_ge(small_hi, 1)
                        dve.tensor_tensor(wr_lo[:, :], wr_in[:, :], wr_hi[:, :], ALU.subtract)
                        dve.tensor_tensor(xwq_lo[:, :], w_in[:, 7, :], xwq_hi[:, :], ALU.subtract).then_inc(small_lo, 1)
                settle()
                dve.sem_clear(dve_step)
                steps_done[0] = 0

            run_phases(dve, body)

_INS = ["x", "ctx_1024", "L0_attn_Wq", "L0_attn_Wk", "L0_attn_Wv", "L0_attn_Wo", "L0_attn_gamma", "L0_attn_beta",
        "L0_xattn_Wk", "L0_xattn_Wv", "L0_xattn_bv", "L0_xattn_Wq", "L0_xattn_bq", "L0_xattn_Wo", "L0_xattn_bo",
        "L0_ffn_Wr", "L0_ffn_br", "L0_ffn_W1", "L0_ffn_b1", "L0_ffn_W2", "L0_ffn_b2"]
_OUTS = [((B, S, E), "float32")]


def kernel(**inputs):
    import numpy as _np
    import concourse.bacc as _bacc
    from concourse import mybir as _mybir
    from concourse.bass_utils import run_bass_kernel_spmd as _run

    nc = _bacc.Bacc("TRN2", target_bir_lowering=False, num_devices=1)
    arrays, args = {}, []
    for name in _INS:
        a = _np.ascontiguousarray(inputs[name])
        arrays[f"in_{name}_dram"] = a
        args.append(nc.dram_tensor(f"in_{name}_dram", a.shape, _mybir.dt.from_np(a.dtype), kind="ExternalInput").ap())
    for i, (shape, dtype) in enumerate(_OUTS):
        dt = _mybir.dt.from_np(_np.dtype(dtype))
        args.append(nc.dram_tensor(f"out_{i}_dram", shape, dt, kind="ExternalOutput").ap())
    bass_decoder_layer(nc, *args)
    r = _run(nc, [arrays], core_ids=[0])
    return r.results[0]["out_0_dram"]
```
